# Optimizing a Trainium2 kernel written in Bass

```python
import numpy as np
import jax
import jax.numpy as jnp

def _softmax(x, axis=-1):
    return jax.nn.softmax(x, axis=axis)

def _gelu(x):
    return jax.nn.gelu(x, approximate=True)

def _silu(x):
    return jax.nn.silu(x)

def _sigmoid(x):
    return jax.nn.sigmoid(x)

def _layernorm(x, axis=-1, eps=1e-05):
    m = jnp.mean(x, axis=axis, keepdims=True)
    v = jnp.var(x, axis=axis, keepdims=True)
    return (x - m) / jnp.sqrt(v + eps)

def _scatter_add(tgt, idx, src, axis=0):
    return tgt.at[idx].add(src)

def _segment_sum(src, seg, n):
    return jax.ops.segment_sum(src, seg, n)
kernel_name = 'mk_decoder_preln_d1_seqx_r4_bcca39'

def setup_inputs(seed: int=0):
    np.random.seed(seed)
    _w = jnp.asarray

    def _rec_inputs():
        import jax
        import jax.numpy as jnp
        _rk = jax.random.key(seed)
        x = 7.22e-05 + 1 * jax.random.normal(jax.random.fold_in(_rk, 1), (4, 512, 512), jnp.float32)
        _lenS = 512 - jax.random.randint(jax.random.fold_in(_rk, 7), (4,), 0, max(1, 512 // 4) + 1, jnp.int32)
        _lenS2 = 512 - jax.random.randint(jax.random.fold_in(_rk, 8), (4,), 0, max(1, 512 // 4) + 1, jnp.int32)
        _ctx_1024P = jax.random.normal(jax.random.fold_in(_rk, 11), (4, 16, 256), jnp.float32)
        _ctx_1024c = jax.random.dirichlet(jax.random.fold_in(_rk, 511), 0.3 * jnp.ones((16,), jnp.float32), (4, 512))
        _ctx_1024t = jnp.einsum('bsk,bkd->bsd', _ctx_1024c, _ctx_1024P)
        _ctx_1024t = _ctx_1024t * jax.lax.rsqrt(jnp.mean(jnp.square(_ctx_1024t)) + 1e-12) * 0.953939
        ctx_1024 = 2.81802e-05 + 1.00001 * (_ctx_1024t + 0.3 * jax.random.normal(jax.random.fold_in(_rk, 611), (4, 512, 256), jnp.float32))
        return (x, ctx_1024)
    x, ctx_1024 = _rec_inputs()

    def _L0_attn_setup():
        import jax, jax.numpy as jnp
        import numpy as np
        NUM_HEADS = 16
        ROPE_BASE = 10000.0

        def build_rope_cache(seq_len, n_elem):
            theta = 1.0 / ROPE_BASE ** (jnp.arange(0, n_elem, 2, dtype=jnp.float32) / n_elem)
            idx_theta = jnp.outer(jnp.arange(seq_len, dtype=jnp.float32), theta)
            return jnp.stack([jnp.cos(idx_theta), jnp.sin(idx_theta)], axis=-1)

        def apply_rope(x, rope):
            B, H, T, D = x.shape
            xt = x.transpose(0, 2, 1, 3)
            xs = xt.reshape(B, T, H, D // 2, 2)
            rc = rope[:T].reshape(1, T, 1, D // 2, 2)
            cos, sin = (rc[..., 0], rc[..., 1])
            x0, x1 = (xs[..., 0], xs[..., 1])
            out = jnp.stack([x0 * cos - x1 * sin, x1 * cos + x0 * sin], axis=-1)
            return out.reshape(B, T, H, D).transpose(0, 2, 1, 3)
        key = jax.random.key(seed)
        k1, k2, k3 = jax.random.split(key, 3)
        B, T, C = (2, 512, 512)
        x = jax.random.normal(k1, (B, T, C), dtype=jnp.float32)
        w_atten = jax.random.normal(k2, (3 * C, C), dtype=jnp.float32) * (1.0 / np.sqrt(C))
        w_proj = jax.random.normal(k3, (C, C), dtype=jnp.float32) * (1.0 / np.sqrt(C))
        return {'x': x, 'w_atten': w_atten, 'w_proj': w_proj}
    _L0_attn_all = _L0_attn_setup()
    _L0_attn_in = {k: v for k, v in _L0_attn_all.items() if k in ('w_atten', 'w_proj')}
    del _L0_attn_all

    def _L0_xattn_setup():
        import jax, jax.numpy as jnp
        import numpy as np
        key = jax.random.key(seed)
        ks = jax.random.split(key, 6)
        B, L, N, C, D = (8, 128, 512, 256, 128)
        return {'teacher_logits': jax.random.normal(ks[0], (B, L, N), dtype=jnp.float32), 'teacher_features': jax.random.normal(ks[1], (B, N, C), dtype=jnp.float32), 'Wq': jax.random.normal(ks[2], (D, C), dtype=jnp.float32) * (1.0 / np.sqrt(C)), 'bq': jnp.zeros((D,), dtype=jnp.float32), 'Wk': jax.random.normal(ks[3], (D, C), dtype=jnp.float32) * (1.0 / np.sqrt(C)), 'bk': jnp.zeros((D,), dtype=jnp.float32)}
    _L0_xattn_all = _L0_xattn_setup()
    _L0_xattn_in = {k: v for k, v in _L0_xattn_all.items() if k in ('Wq', 'bq', 'Wk', 'bk')}
    del _L0_xattn_all

    def _L0_ffn_setup():
        import jax, jax.numpy as jnp
        import numpy as np
        E = 8
        TOP_K = 2
        D = 512
        DE = 352
        DS = 704
        B, S = (2, 512)
        key = jax.random.key(seed)
        ks = jax.random.split(key, 8)
        std = 0.02
        return {'x': jax.random.normal(ks[0], (B, S, D), jnp.float32), 'W_router': jax.random.normal(ks[1], (D, E), jnp.float32) * std, 'We_gate': jax.random.normal(ks[2], (E, D, DE), jnp.float32) * std, 'We_up': jax.random.normal(ks[3], (E, D, DE), jnp.float32) * std, 'We_down': jax.random.normal(ks[4], (E, DE, D), jnp.float32) * std, 'Ws_gate': jax.random.normal(ks[5], (D, DS), jnp.float32) * std, 'Ws_up': jax.random.normal(ks[6], (D, DS), jnp.float32) * std, 'Ws_down': jax.random.normal(ks[7], (DS, D), jnp.float32) * std}
    _L0_ffn_all = _L0_ffn_setup()
    _L0_ffn_in = {k: v for k, v in _L0_ffn_all.items() if k in ('W_router', 'We_gate', 'We_up', 'We_down', 'Ws_gate', 'Ws_up', 'Ws_down')}
    del _L0_ffn_all
    return {'x': x, 'ctx_1024': ctx_1024, 'L0_attn_w_atten': _L0_attn_in['w_atten'], 'L0_attn_w_proj': _L0_attn_in['w_proj'], 'L0_xattn_Wq': _L0_xattn_in['Wq'], 'L0_xattn_bq': _L0_xattn_in['bq'], 'L0_xattn_Wk': _L0_xattn_in['Wk'], 'L0_xattn_bk': _L0_xattn_in['bk'], 'L0_ffn_W_router': _L0_ffn_in['W_router'], 'L0_ffn_We_gate': _L0_ffn_in['We_gate'], 'L0_ffn_We_up': _L0_ffn_in['We_up'], 'L0_ffn_We_down': _L0_ffn_in['We_down'], 'L0_ffn_Ws_gate': _L0_ffn_in['Ws_gate'], 'L0_ffn_Ws_up': _L0_ffn_in['Ws_up'], 'L0_ffn_Ws_down': _L0_ffn_in['Ws_down']}

def reference(x, ctx_1024, L0_attn_w_atten, L0_attn_w_proj, L0_xattn_Wq, L0_xattn_bq, L0_xattn_Wk, L0_xattn_bk, L0_ffn_W_router, L0_ffn_We_gate, L0_ffn_We_up, L0_ffn_We_down, L0_ffn_Ws_gate, L0_ffn_Ws_up, L0_ffn_Ws_down):
    import jax
    import jax.numpy as jnp

    def _L0_attn_ref(x, w_atten, w_proj):
        import jax, jax.numpy as jnp
        import numpy as np
        NUM_HEADS = 16
        ROPE_BASE = 10000.0

        def build_rope_cache(seq_len, n_elem):
            theta = 1.0 / ROPE_BASE ** (jnp.arange(0, n_elem, 2, dtype=jnp.float32) / n_elem)
            idx_theta = jnp.outer(jnp.arange(seq_len, dtype=jnp.float32), theta)
            return jnp.stack([jnp.cos(idx_theta), jnp.sin(idx_theta)], axis=-1)

        def apply_rope(x, rope):
            B, H, T, D = x.shape
            xt = x.transpose(0, 2, 1, 3)
            xs = xt.reshape(B, T, H, D // 2, 2)
            rc = rope[:T].reshape(1, T, 1, D // 2, 2)
            cos, sin = (rc[..., 0], rc[..., 1])
            x0, x1 = (xs[..., 0], xs[..., 1])
            out = jnp.stack([x0 * cos - x1 * sin, x1 * cos + x0 * sin], axis=-1)
            return out.reshape(B, T, H, D).transpose(0, 2, 1, 3)
        B, T, C = x.shape
        H = NUM_HEADS
        D = C // H
        qkv = x @ w_atten.T
        q, k, v = jnp.split(qkv, 3, axis=2)
        q = q.reshape(B, T, H, D).transpose(0, 2, 1, 3)
        k = k.reshape(B, T, H, D).transpose(0, 2, 1, 3)
        v = v.reshape(B, T, H, D).transpose(0, 2, 1, 3)
        rope = build_rope_cache(T, D)
        q = apply_rope(q, rope)
        k = apply_rope(k, rope)
        att = jnp.einsum('bhqd,bhkd->bhqk', q, k) * (1.0 / jnp.sqrt(jnp.float32(D)))
        causal = jnp.tril(jnp.ones((T, T), dtype=bool))
        att = jnp.where(causal[None, None], att, jnp.float32(-jnp.inf))
        att = jax.nn.softmax(att, axis=-1)
        y = jnp.einsum('bhqk,bhkd->bhqd', att, v)
        y = y.transpose(0, 2, 1, 3).reshape(B, T, C)
        return y @ w_proj.T

    def _L0_xattn_ref(teacher_logits, teacher_features, Wq, bq, Wk, bk):
        import jax, jax.numpy as jnp
        import numpy as np
        query = jnp.einsum('bnc,dc->bnd', teacher_features, Wq) + bq
        key = jnp.einsum('bnc,dc->bnd', teacher_features, Wk) + bk
        energy = jnp.einsum('bnd,bmd->bnm', query, key)
        attention = jax.nn.softmax(energy, axis=-1)
        x_m = jnp.einsum('bln,bmn->blm', teacher_logits, attention)
        return x_m

    def _L0_ffn_ref(x, W_router, We_gate, We_up, We_down, Ws_gate, Ws_up, Ws_down):
        import jax, jax.numpy as jnp
        import numpy as np
        E = 8
        TOP_K = 2
        D = 512
        DE = 352
        DS = 704
        B, S = (2, 512)
        b, s, d = x.shape
        shared = jax.nn.silu(x @ Ws_gate) * (x @ Ws_up) @ Ws_down
        scores = jax.nn.softmax(x @ W_router, axis=-1)
        topk_vals, topk_idx = jax.lax.top_k(scores, TOP_K)
        onehot = jax.nn.one_hot(topk_idx, E, dtype=x.dtype)
        combine = jnp.einsum('bsk,bske->bse', topk_vals, onehot)
        combine = combine.reshape(b * s, E)
        xf = x.reshape(b * s, d)
        h = jax.nn.silu(jnp.einsum('td,edh->eth', xf, We_gate)) * jnp.einsum('td,edh->eth', xf, We_up)
        y_all = jnp.einsum('eth,ehd->etd', h, We_down)
        routed = jnp.einsum('etd,te->td', y_all, combine)
        return routed.reshape(b, s, d) + shared
    x = x + _L0_attn_ref(_layernorm(x, axis=-1), L0_attn_w_atten, L0_attn_w_proj)
    x = x + _L0_xattn_ref(_layernorm(x, axis=-1), ctx_1024, L0_xattn_Wq, L0_xattn_bq, L0_xattn_Wk, L0_xattn_bk)
    x = x + _L0_ffn_ref(_layernorm(x, axis=-1), L0_ffn_W_router, L0_ffn_We_gate, L0_ffn_We_up, L0_ffn_We_down, L0_ffn_Ws_gate, L0_ffn_Ws_up, L0_ffn_Ws_down)
    return x

_drawn_inputs = setup_inputs


def setup_inputs(seed=0):
    import zlib

    import numpy as np

    out = dict(_drawn_inputs(seed))
    spreads = {'L0_xattn_bq': (0.0, 0.1), 'L0_xattn_bk': (0.0, 2.0)}
    factors = {'L0_ffn_W_router': 7.125,
     'L0_ffn_We_gate': 6.398,
     'L0_ffn_We_up': 6.244,
     'L0_ffn_We_down': 6.263,
     'L0_ffn_Ws_gate': 8.0,
     'L0_ffn_Ws_up': 8.0,
     'L0_ffn_Ws_down': 8.0}
    for name, (base, spread) in spreads.items():
        noise = np.random.default_rng([zlib.crc32(name.encode()), seed]).standard_normal(out[name].shape)
        drawn = base * np.exp(spread * noise) if base else spread * noise
        out[name] = jnp.asarray(drawn.astype(out[name].dtype))
    for name, factor in factors.items():
        out[name] = (out[name] * factor).astype(out[name].dtype)
    return out
```

```python
from contextlib import ExitStack

import numpy as np

import concourse.bass as bass
from concourse import mybir

P = 128
F32 = mybir.dt.float32
ALU = mybir.AluOpType
ACT = mybir.ActivationFunctionType
AX_X = mybir.AxisListType.X

BATCHES, TOKENS, DIM = 4, 512, 512
CTX = 256
HEADS, HDIM = 16, 32
EXPERTS, EDIM = 8, 352
SHARED = 2
SLOTS = EXPERTS + SHARED
TT = TOKENS // P
TILES = BATCHES * TT
CC = DIM // P
GROUPS = HEADS * HDIM // P
GH = P // HDIM
STEPS = GROUPS * TT
HCHUNKS = [(f * P, min(P, EDIM - f * P)) for f in range((EDIM + P - 1) // P)]
EPS = 1e-5
SCALE = float(HDIM) ** -0.5
MASKED = -1e30
LOWEST = -3e38


def build(nc, x, ctxT, waT, wpT, wqT, wkT, bq, bk, wr, wg, wu, wd, cosT, sinT, out):
    with ExitStack() as stack:
        def sb(name, shape, dt=F32):
            return stack.enter_context(nc.sbuf_tensor(name, shape, dt))

        def sem(name):
            return stack.enter_context(nc.semaphore(name))

        acc = sb("acc", [P, TILES, DIM])
        xn3T = sb("xn3T", [P, CC, BATCHES * TOKENS])
        comb = sb("comb", [P, SLOTS, TILES])
        ctx_sb = sb("ctx_sb", [P, CTX // P, TOKENS])
        wa_sb = sb("wa_sb", [P, CC, 3 * DIM])
        wp_sb = sb("wp_sb", [P, CC, DIM])
        wq_sb = sb("wq_sb", [P, CTX // P, P])
        wk_sb = sb("wk_sb", [P, CTX // P, P])
        wr_sb = sb("wr_sb", [P, CC, EXPERTS])
        bias_sb = sb("bias_sb", [P, 2])
        cos_sb = sb("cos_sb", [P, TOKENS])
        sin_sb = sb("sin_sb", [P, TOKENS])
        ident = sb("ident", [P, P])
        mask = sb("mask", [P, TOKENS])
        iota8 = sb("iota8", [P, TT, EXPERTS])
        stats = sb("stats", [P, TT, 6])
        mv = sb("mv", [P, TT, 2])
        veps = sb("veps", [P, TT])
        rstd = sb("rstd", [P, TT])
        power = sb("power", [P, TT])
        xn = sb("xn", [P, TT, DIM])
        xnT = sb("xnT", [P, CC, TOKENS])
        v_sb = sb("v_sb", [P, TT, DIM])
        qz = sb("qz", [P, 2, GH, TOKENS])
        kr = sb("kr", [P, 2, TOKENS])
        rope_sw = sb("rope_sw", [P, TOKENS])
        rope_c = sb("rope_c", [P, TOKENS])
        probs = sb("probs", [P, 2, GH, TOKENS])
        probsT = sb("probsT", [P, 2, GH, TOKENS])
        mx = sb("mx", [P, 2, GH])
        nb = sb("nb", [P, 2, GH])
        sums = sb("sums", [P, 2, GH])
        rsum = sb("rsum", [P, 2, GH])
        yT = sb("yT", [P, GROUPS, TOKENS])
        q2 = sb("q2", [P, TOKENS])
        k2 = sb("k2", [P, TOKENS])
        attT = probsT[:, 1, :, :]
        r_sc = sb("r_sc", [P, TT, EXPERTS])
        r_t = sb("r_t", [P, TT, EXPERTS])
        r_oh = sb("r_oh", [P, TT, EXPERTS])
        r_oh2 = sb("r_oh2", [P, TT, EXPERTS])
        r_m = sb("r_m", [P, TT])
        wg_sb = [wa_sb[:, 0, 0:4 * EDIM].rearrange("p (c n) -> p c n", c=CC),
                 wa_sb[:, 1, 0:4 * EDIM].rearrange("p (c n) -> p c n", c=CC)]
        wu_sb = [wa_sb[:, 2, 0:4 * EDIM].rearrange("p (c n) -> p c n", c=CC),
                 wa_sb[:, 3, 0:4 * EDIM].rearrange("p (c n) -> p c n", c=CC)]
        wd_sb = [probs[:, 0, 0:3, :], probs[:, 1, 0:3, :]]
        sg = [qz[:, 0, 0, :], qz[:, 0, 1, :]]
        hT = [probsT[:, 0, 0:3, :], probsT[:, 1, 0:3, :]]

        ps = stack.enter_context(nc.psum_tensor("ps", [P, 8, 512], F32))
        O_BANK, QK_BANK = 6, 7

        x_loaded = sem("x_loaded")
        w_loaded = sem("w_loaded")
        ctx_loaded = sem("ctx_loaded")
        ctx_used = sem("ctx_used")
        consts = sem("consts")
        zeroed = sem("zeroed")
        ln_stats = sem("ln_stats")
        ln_var = sem("ln_var")
        ln_rstd = sem("ln_rstd")
        ln_xn = sem("ln_xn")
        ln_tr = sem("ln_tr")
        ln_xnT = sem("ln_xnT")
        v_mm = sem("v_mm")
        v_done = sem("v_done")
        qk_mm = sem("qk_mm")
        qk_used = sem("qk_used")
        rope_link = sem("rope_link")
        rope_done = sem("rope_done")
        s_mm = sem("s_mm")
        s_masked = sem("s_masked")
        nb_done = sem("nb_done")
        exp_done = sem("exp_done")
        rsum_done = sem("rsum_done")
        p_ready = sem("p_ready")
        pT_mm = sem("pT_mm")
        pT_done = sem("pT_done")
        pv_mm = sem("pv_mm")
        yT_done = sem("yT_done")
        proj_mm = sem("proj_mm")
        proj_added = sem("proj_added")
        qk2_mm = sem("qk2_mm")
        qk2_done = sem("qk2_done")
        e_mm = sem("e_mm")
        e_max = sem("e_max")
        e_nb = sem("e_nb")
        e_exp = sem("e_exp")
        e_rsum = sem("e_rsum")
        a_ready = sem("a_ready")
        aT_mm = sem("aT_mm")
        aT_done = sem("aT_done")
        xm_mm = sem("xm_mm")
        xm_added = sem("xm_added")
        xn3_copied = sem("xn3_copied")
        r_mm = sem("r_mm")
        r_link = sem("r_link")
        r_shift = sem("r_shift")
        r_exp = sem("r_exp")
        e_loaded = [sem("e_loaded0"), sem("e_loaded1")]
        e_used = [sem("e_used0"), sem("e_used1")]
        gu_mm = sem("gu_mm")
        sg_done = sem("sg_done")
        h_done = sem("h_done")
        y_mm = sem("y_mm")
        y_added = sem("y_added")
        stored = sem("stored")

        waited = sem("waited")

        def pass_wait(eng):
            eng.nop().then_inc(waited, 1)

        W_LOADS = 10
        ROUTER_LINKS = 17
        x_v = x.rearrange("(b t p) d -> b p t d", p=P, t=TT)
        out_v = out.rearrange("(b t p) d -> b p t d", p=P, t=TT)
        ctx_v = ctxT.rearrange("b (c p) n -> p (b c) n", p=P)
        NCTX = CTX // P

        block = stack.enter_context(nc.Block())

        @block.sync
        def _(sp):
            sp.dma_start(acc[:, 0:TT, :], x_v[0]).then_inc(x_loaded, 16)
            loads = [(wa_sb[:], waT.rearrange("(c p) n -> p c n", p=P)), (cos_sb[:], cosT), (sin_sb[:], sinT),
                     (wp_sb[:], wpT.rearrange("(c p) n -> p c n", p=P)),
                     (wq_sb[:], wqT.rearrange("(c p) n -> p c n", p=P)),
                     (wk_sb[:], wkT.rearrange("(c p) n -> p c n", p=P)),
                     (wr_sb[:], wr.rearrange("(c p) n -> p c n", p=P)),
                     (bias_sb[:, 0:1], bq), (bias_sb[:, 1:2], bk)]
            for dst, src in loads:
                sp.dma_start(dst, src).then_inc(w_loaded, 16)
            sp.dma_start(acc[:, TT:TILES, :], x[TT * P:, :].rearrange("(t p) d -> p t d", p=P)).then_inc(w_loaded, 16)
            with sp.Fori(0, BATCHES) as b:
                sp.wait_ge(ctx_used, b + 1)
                sp.dma_start(ctx_sb[:], ctx_v[:, bass.ds(b * NCTX, NCTX), :]).then_inc(ctx_loaded, 16)
            sp.wait_ge(r_link, BATCHES * ROUTER_LINKS)
            with sp.Fori(0, SLOTS // 2) as pair:
                for k in range(2):
                    sp.wait_ge(e_used[k], pair + 1)
                    e = pair * 2 + k
                    for dst, src in ((wg_sb[k], wg), (wu_sb[k], wu)):
                        sp.dma_start(dst, src.rearrange("(e c p) n -> p e c n", p=P, c=CC)[:, bass.ds(e, 1), :, :]
                                     .rearrange("p e c n -> p (e c) n")).then_inc(e_loaded[k], 16)
                    for f, (f0, fn) in enumerate(HCHUNKS):
                        sp.dma_start(wd_sb[k][0:fn, f, :], wd[bass.ds(e * EDIM + f0, fn), :]).then_inc(e_loaded[k], 16)
            sp.wait_ge(y_added, 4 + SLOTS * TILES)
            for b in range(BATCHES):
                sp.dma_start(out_v[b], acc[:, b * TT:(b + 1) * TT, :]).then_inc(stored, 16)
            sp.wait_ge(stored, 16 * BATCHES)

        @block.gpsimd
        def _(pool):
            nc.gpsimd.memset(ident[:], 0.0).then_inc(zeroed, 1)
            nc.gpsimd.memset(mask[:], 0.0).then_inc(zeroed, 1)
            nc.gpsimd.memset(power[:], -0.5).then_inc(zeroed, 1)
            pool.wait_ge(zeroed, 3)
            nc.gpsimd.affine_select(out=ident[:], in_=ident[:], compare_op=ALU.not_equal, fill=1.0, base=0,
                                    pattern=[[-1, P]], channel_multiplier=1).then_inc(consts, 1)
            diag = mask[:, TOKENS - P:TOKENS]
            nc.gpsimd.affine_select(out=diag, in_=diag, compare_op=ALU.is_ge, fill=MASKED, base=0,
                                    pattern=[[-1, P]], channel_multiplier=1).then_inc(consts, 1)
            nc.gpsimd.iota(iota8[:], pattern=[[0, TT], [1, EXPERTS]], base=0, channel_multiplier=0,
                           allow_small_or_imprecise_dtypes=True).then_inc(consts, 1)
            with pool.Fori(0, BATCHES) as b:
                for k in range(3):
                    pool.wait_ge(ln_var, b * 3 + k + 1)
                    nc.gpsimd.tensor_tensor(rstd[:], veps[:], power[:], ALU.pow).then_inc(ln_rstd, 1)
                pool.wait_ge(ln_xnT, b * (3 * TT) + 3 * TT)
                nc.gpsimd.tensor_copy(xn3T[:, :, bass.ds(b * TOKENS, TOKENS)], xnT[:]).then_inc(xn3_copied, 1)

        @block.scalar
        def _(act):
            act.wait_ge(w_loaded, 16 * W_LOADS)

            def evacuate_ln(b, k):
                for t in range(TT):
                    act.wait_ge(ln_tr, b * (3 * TT) + k * TT + t + 1)
                    nc.scalar.copy(xnT[:, :, t * P:(t + 1) * P],
                                   ps[:, 4 + t % 2, :].rearrange("p (c n) -> p c n", c=CC)).then_inc(ln_xnT, 1)

            with act.Fori(0, BATCHES) as b:
                act.wait_ge(xn3_copied, b + 1)
                evacuate_ln(b, 0)
                for t in range(TT):
                    act.wait_ge(v_mm, b * TT + t + 1)
                    nc.scalar.copy(v_sb[:, t, :], ps[:, 6 + t % 2, :]).then_inc(v_done, 1)
                for r in range(STEPS + 1):
                    if r >= 1:
                        n, w = r - 1, ((r - 1) % TT + 1) * P
                        if n >= 2:
                            act.wait_ge(pv_mm, b * STEPS + n - 1)
                        for h in range(GH):
                            act.wait_ge(pT_mm, b * HEADS * TT + GH * n + h + 1)
                            nc.scalar.copy(probsT[:, n % 2, h, 0:w], ps[:, 4 + h % 2, 0:w]).then_inc(pT_done, 1)
                    if r < STEPS:
                        w = (r % TT + 1) * P
                        act.wait_ge(nb_done, b * STEPS + r + 1)
                        for h in range(GH):
                            pr = probs[:, r % 2, h, 0:w]
                            nc.scalar.activation(pr, pr, ACT.Exp, bias=nb[:, r % 2, h:h + 1], scale=SCALE,
                                                 accum_out=sums[:, r % 2, h:h + 1]).then_inc(exp_done, 1)
                    if r >= 1 and r % TT == 0:
                        g = r // TT - 1
                        act.wait_ge(pv_mm, b * STEPS + r)
                        nc.scalar.copy(yT[:, g, :], ps[:, O_BANK, :]).then_inc(yT_done, 1)
                for i, dst in enumerate((q2, k2)):
                    act.wait_ge(qk2_mm, b * 2 + i + 1)
                    nc.scalar.activation(dst[:], ps[:, 6 + i, :], ACT.Identity, bias=bias_sb[:, i:i + 1],
                                         scale=1.0).then_inc(qk2_done, 1)
                for t in range(TT):
                    act.wait_ge(e_nb, b * TT + t + 1)
                    nc.scalar.activation(probs[:, 0, t, :], ps[:, t, :], ACT.Exp, bias=nb[:, 0, t:t + 1],
                                         scale=1.0, accum_out=sums[:, 0, t:t + 1]).then_inc(e_exp, 1)
                evacuate_ln(b, 1)
                for t in range(TT):
                    act.wait_ge(aT_mm, b * TT + t + 1)
                    nc.scalar.copy(attT[:, :, t * P:(t + 1) * P],
                                   ps[:, 4 + t % 2, :].rearrange("p (c n) -> p c n", c=TT)).then_inc(aT_done, 1)
                evacuate_ln(b, 2)
                act.wait_ge(r_shift, b + 1)
                nc.scalar.activation(r_sc[:], r_t[:], ACT.Exp).then_inc(r_exp, 1)
            with act.Fori(0, SLOTS // 2) as pair:
                for q in range(2 * BATCHES * len(HCHUNKS)):
                    fn = HCHUNKS[q % len(HCHUNKS)][1]
                    act.wait_ge(gu_mm, pair * (2 * BATCHES * len(HCHUNKS)) + q + 1)
                    nc.scalar.activation(sg[q % 2][0:fn, :], ps[0:fn, 2 * (q % 2), :], ACT.Silu).then_inc(sg_done, 1)

        @block.tensor
        def _(pe):
            pe.nop().then_inc(ctx_used, 1)
            pe.wait_ge(consts, 3)
            pe.wait_ge(w_loaded, 16 * W_LOADS)

            def transpose_ln(b, k):
                for t in range(TT):
                    pe.wait_ge(ln_xn, b * (3 * TT) + k * TT + t + 1)
                    if t >= 2:
                        pe.wait_ge(ln_xnT, b * (3 * TT) + k * TT + t - 1)
                    for c in range(CC):
                        last = nc.tensor.transpose(ps[:, 4 + t % 2, c * P:(c + 1) * P], xn[:, t, c * P:(c + 1) * P],
                                                   ident[:])
                    last.then_inc(ln_tr, 1)

            def project_qk(b, g):
                for i in range(2):
                    e = 2 * g + i
                    if e >= 1:
                        pe.wait_ge(qk_used, b * 2 * GROUPS + e)
                    for c in range(CC):
                        col = i * DIM + g * P
                        last = nc.tensor.matmul(ps[:, QK_BANK, :], wa_sb[:, c, col:col + P], xnT[:, c, :],
                                                start=(c == 0), stop=(c == CC - 1))
                    last.then_inc(qk_mm, 1)

            def scores(b, n):
                g, i = divmod(n, TT)
                w = (i + 1) * P
                pe.wait_ge(rope_done, b * 2 * GROUPS + 2 * g + 2)
                for h in range(GH):
                    if n >= 1:
                        pe.wait_ge(s_masked, b * HEADS * TT + GH * (n - 1) + h + 1)
                    nc.tensor.matmul(ps[:, h, 0:w], qz[:, g % 2, h, i * P:(i + 1) * P], kr[:, g % 2, 0:w],
                                     start=True, stop=True).then_inc(s_mm, 1)

            def weigh(b, n):
                g, i = divmod(n, TT)
                for h in range(GH):
                    pe.wait_ge(p_ready, b * HEADS * TT + GH * n + h + 1)
                    if n or h >= 2:
                        pe.wait_ge(pT_done, b * HEADS * TT + GH * n + h - 1)
                    for j in range(i + 1):
                        last = nc.tensor.transpose(ps[:, 4 + h % 2, j * P:(j + 1) * P],
                                                   probs[:, n % 2, h, j * P:(j + 1) * P], ident[:])
                    last.then_inc(pT_mm, 1)
                pe.wait_ge(pT_done, b * HEADS * TT + GH * n + GH)
                if i == 0 and g >= 1:
                    pe.wait_ge(yT_done, b * GROUPS + g)
                for j in range(i + 1):
                    for h in range(GH):
                        last = nc.tensor.matmul(ps[h * HDIM:(h + 1) * HDIM, O_BANK, i * P:(i + 1) * P],
                                                v_sb[:, j, g * P + h * HDIM:g * P + (h + 1) * HDIM],
                                                probsT[:, n % 2, h, j * P:(j + 1) * P],
                                                start=(j == 0), stop=(j == i), skip_group_check=True)
                last.then_inc(pv_mm, 1)

            with pe.Fori(0, BATCHES) as b:
                transpose_ln(b, 0)
                for t in range(TT):
                    pe.wait_ge(ln_xnT, b * (3 * TT) + t + 1)
                    if t >= 2:
                        pe.wait_ge(v_done, b * TT + t - 1)
                    for c in range(CC):
                        last = nc.tensor.matmul(ps[:, 6 + t % 2, :], xnT[:, c, t * P:(t + 1) * P],
                                                wa_sb[:, c, 2 * DIM:3 * DIM], start=(c == 0), stop=(c == CC - 1))
                    last.then_inc(v_mm, 1)
                pe.wait_ge(v_done, b * TT + TT)
                project_qk(b, 0)
                for r in range(STEPS + 1):
                    if r < STEPS:
                        scores(b, r)
                    if r % TT == 2 and r // TT + 1 < GROUPS:
                        project_qk(b, r // TT + 1)
                    if r >= 1:
                        weigh(b, r - 1)
                pe.wait_ge(yT_done, b * GROUPS + GROUPS)
                for t in range(TT):
                    for c in range(CC):
                        last = nc.tensor.matmul(ps[:, t, :], yT[:, c, t * P:(t + 1) * P], wp_sb[:, c, :],
                                                start=(c == 0), stop=(c == CC - 1))
                    last.then_inc(proj_mm, 1)
                pe.wait_ge(ctx_loaded, b * 16 + 16)
                for i, w in enumerate((wq_sb, wk_sb)):
                    for c in range(NCTX):
                        last = nc.tensor.matmul(ps[:, 6 + i, :], w[:, c, :], ctx_sb[:, c, :],
                                                start=(c == 0), stop=(c == NCTX - 1))
                    last.then_inc(qk2_mm, 1)
                pe.wait_ge(qk2_done, b * 2 + 2)
                for t in range(TT):
                    pe.wait_ge(proj_added, b * TT + t + 1)
                    nc.tensor.matmul(ps[:, t, :], q2[:, t * P:(t + 1) * P], k2[:], start=True, stop=True)\
                        .then_inc(e_mm, 1)
                pe.nop().then_inc(ctx_used, 1)
                transpose_ln(b, 1)
                for t in range(TT):
                    pe.wait_ge(a_ready, b * TT + t + 1)
                    if t < 2:
                        pe.wait_ge(ln_xnT, b * (3 * TT) + 2 * TT)
                    else:
                        pe.wait_ge(aT_done, b * TT + t - 1)
                    for c in range(TT):
                        last = nc.tensor.transpose(ps[:, 4 + t % 2, c * P:(c + 1) * P],
                                                   probs[:, 0, t, c * P:(c + 1) * P], ident[:])
                    last.then_inc(aT_mm, 1)
                pe.wait_ge(aT_done, b * TT + TT)
                for t in range(TT):
                    for c in range(TT):
                        last = nc.tensor.matmul(ps[:, t, :], xnT[:, c, t * P:(t + 1) * P], attT[:, c, :],
                                                start=(c == 0), stop=(c == TT - 1))
                    last.then_inc(xm_mm, 1)
                transpose_ln(b, 2)
                pe.wait_ge(ln_xnT, b * (3 * TT) + 3 * TT)
                for t in range(TT):
                    for c in range(CC):
                        last = nc.tensor.matmul(ps[:, QK_BANK, t * EXPERTS:(t + 1) * EXPERTS],
                                                xnT[:, c, t * P:(t + 1) * P], wr_sb[:, c, :],
                                                start=(c == 0), stop=(c == CC - 1))
                last.then_inc(r_mm, 1)
                pe.wait_ge(r_shift, b + 1)

            NF = len(HCHUNKS)

            def hidden(pair, k, tg):
                for f, (f0, fn) in enumerate(HCHUNKS):
                    q = (k * BATCHES + tg) * NF + f
                    pe.wait_ge(h_done, pair * (2 * BATCHES * NF) + q + 1)
                    for w, bank in ((wg_sb[k], 2 * (q % 2)), (wu_sb[k], 2 * (q % 2) + 1)):
                        for c in range(CC):
                            last = nc.tensor.matmul(ps[0:fn, bank, :], w[:, c, f0:f0 + fn],
                                                    xn3T[:, c, tg * TOKENS:(tg + 1) * TOKENS],
                                                    start=(c == 0), stop=(c == CC - 1))
                    last.then_inc(gu_mm, 1)

            def down(pair, n):
                k, tg = divmod(n, BATCHES)
                pe.wait_ge(h_done, pair * (2 * BATCHES * NF) + n * NF + NF + 2)
                for t in range(TT):
                    d = n * TT + t
                    pe.wait_ge(y_added, pair * (2 * TILES) + d + 1)
                    for f, (f0, fn) in enumerate(HCHUNKS):
                        last = nc.tensor.matmul(ps[:, 4 + t, :], hT[n % 2][0:fn, f, t * P:(t + 1) * P],
                                                wd_sb[k][0:fn, f, :], start=(f == 0), stop=(f == NF - 1))
                    last.then_inc(y_mm, 1)

            pe.wait_ge(xn3_copied, 1 + BATCHES)
            with pe.Fori(0, SLOTS // 2) as pair:
                for n in range(2 * BATCHES + 1):
                    if n < 2 * BATCHES:
                        if n % BATCHES == 0:
                            k = n // BATCHES
                            pe.wait_ge(e_loaded[k], pair * 80 + 80)
                        hidden(pair, n // BATCHES, n % BATCHES)
                    if n >= 1:
                        down(pair, n - 1)

        @block.vector
        def _(dve):
            nc.vector.memset(qz[:], 0.0).then_inc(rope_link, 1)
            nc.vector.memset(comb[:], 1.0).then_inc(rope_link, 1)
            dve.wait_ge(rope_link, 2)
            dve.nop().then_inc(xn3_copied, 1)
            dve.wait_ge(x_loaded, 16)
            dve.wait_ge(consts, 3)
            dve.wait_ge(w_loaded, 16 * W_LOADS)

            def normalise(b, k):
                pass_wait(dve)
                for t in range(TT):
                    nc.vector.bn_stats(stats[:, t, :], acc[:, bass.ds(b * TT + t, 1), :]
                                       .rearrange("p o d -> p (o d)")).then_inc(ln_stats, 1)
                per = 2 * TT
                dve.wait_ge(ln_stats, b * (3 * per) + k * per + TT)
                pass_wait(dve)
                for t in range(TT):
                    nc.vector.bn_aggr(mv[:, t, :], stats[:, t, :]).then_inc(ln_stats, 1)
                dve.wait_ge(ln_stats, b * (3 * per) + k * per + per)
                nc.vector.tensor_scalar(veps[:], mv[:, :, 1], EPS, None, ALU.add).then_inc(ln_var, 1)
                dve.wait_ge(ln_rstd, b * 3 + k + 1)
                for t in range(TT):
                    nc.vector.tensor_scalar(xn[:, t, :], acc[:, bass.ds(b * TT + t, 1), :]
                                            .rearrange("p o d -> p (o d)"), mv[:, t, 0:1], rstd[:, t:t + 1],
                                            ALU.subtract, ALU.mult).then_inc(ln_xn, 1)

            swap = [i ^ 1 for i in range(32)]
            ROPE_LINKS = 3

            def rope(b, g):
                for i in range(2):
                    e = 2 * g + i
                    links = 2 + b * (2 * GROUPS * ROPE_LINKS) + e * ROPE_LINKS
                    raw = ps[:, QK_BANK, :]
                    dve.wait_ge(qk_mm, b * 2 * GROUPS + e + 1)
                    pass_wait(dve)
                    nc.vector.stream_shuffle(rope_sw[:], raw, swap).then_inc(rope_link, 1)
                    nc.vector.tensor_tensor(rope_c[:], raw, cos_sb[:], ALU.mult).then_inc(rope_link, 1)
                    dve.wait_ge(rope_link, links + 2)
                    dve.nop().then_inc(qk_used, 1)
                    nc.vector.tensor_tensor(rope_sw[:], rope_sw[:], sin_sb[:], ALU.mult).then_inc(rope_link, 1)
                    dve.wait_ge(rope_link, links + 3)
                    if i == 1:
                        nc.vector.tensor_tensor(kr[:, g % 2, :], rope_c[:], rope_sw[:], ALU.add).then_inc(rope_done, 1)
                    else:
                        for h in range(GH):
                            rows = slice(h * HDIM, (h + 1) * HDIM)
                            last = nc.vector.tensor_tensor(qz[rows, g % 2, h, :], rope_c[rows, :], rope_sw[rows, :],
                                                           ALU.add)
                        last.then_inc(rope_done, 1)
                    dve.wait_ge(rope_done, b * 2 * GROUPS + e + 1)

            def mask_and_max(b, n):
                i = n % TT
                w = (i + 1) * P
                for h in range(GH):
                    dve.wait_ge(s_mm, b * HEADS * TT + GH * n + h + 1)
                    if n >= 2:
                        dve.wait_ge(pT_mm, b * HEADS * TT + GH * (n - 2) + h + 1)
                    pass_wait(dve)
                    nc.vector.tensor_tensor_reduce(probs[:, n % 2, h, 0:w], ps[:, h, 0:w], mask[:, TOKENS - w:],
                                                   1.0, LOWEST, ALU.add, ALU.max, mx[:, n % 2, h:h + 1])\
                        .then_inc(s_masked, 1)
                dve.wait_ge(s_masked, b * HEADS * TT + GH * n + GH)
                nc.vector.tensor_scalar(nb[:, n % 2, :], mx[:, n % 2, :], -SCALE, None, ALU.mult).then_inc(nb_done, 1)

            def divide(b, n):
                w = (n % TT + 1) * P
                dve.wait_ge(exp_done, b * HEADS * TT + GH * n + GH)
                nc.vector.reciprocal(rsum[:, n % 2, :], sums[:, n % 2, :]).then_inc(rsum_done, 1)
                dve.wait_ge(rsum_done, b * STEPS + n + 1)
                for h in range(GH):
                    pr = probs[:, n % 2, h, 0:w]
                    nc.vector.tensor_scalar(pr, pr, rsum[:, n % 2, h:h + 1], None, ALU.mult).then_inc(p_ready, 1)

            def add_to_residual(b, ready, added):
                for t in range(TT):
                    dve.wait_ge(ready, b * TT + t + 1)
                    tile = acc[:, bass.ds(b * TT + t, 1), :].rearrange("p o d -> p (o d)")
                    nc.vector.tensor_tensor(tile, tile, ps[:, t, :], ALU.add).then_inc(added, 1)
                dve.wait_ge(added, b * TT + TT)

            def route(b):
                count = [0]

                def link(ins):
                    count[0] += 1
                    ins.then_inc(r_link, 1)
                    dve.wait_ge(r_link, b * ROUTER_LINKS + count[0])

                def wide(m):
                    return m.unsqueeze(2).to_broadcast([P, TT, EXPERTS])

                logits = ps[:, QK_BANK, 0:TT * EXPERTS].rearrange("p (t e) -> p t e", e=EXPERTS)
                dve.wait_ge(r_mm, b + 1)
                link(nc.vector.tensor_reduce(r_m[:], logits, AX_X, ALU.max))
                nc.vector.tensor_tensor(r_t[:], logits, wide(r_m[:]), ALU.subtract).then_inc(r_shift, 1)
                dve.wait_ge(r_exp, b + 1)
                link(nc.vector.tensor_reduce(r_m[:], r_sc[:], AX_X, ALU.add))
                link(nc.vector.reciprocal(r_m[:], r_m[:]))
                link(nc.vector.tensor_tensor(r_sc[:], r_sc[:], wide(r_m[:]), ALU.mult))

                def first_of_the_greatest(values, one_hot, scratch):
                    link(nc.vector.tensor_reduce(r_m[:], values, AX_X, ALU.max))
                    link(nc.vector.tensor_tensor(scratch, values, wide(r_m[:]), ALU.is_lt))
                    link(nc.vector.scalar_tensor_tensor(out=scratch, in0=scratch, scalar=float(EXPERTS),
                                                        in1=iota8[:], op0=ALU.mult, op1=ALU.add))
                    link(nc.vector.tensor_reduce(r_m[:], scratch, AX_X, ALU.min))
                    link(nc.vector.tensor_tensor(one_hot, iota8[:], wide(r_m[:]), ALU.is_equal))

                first_of_the_greatest(r_sc[:], r_oh[:], r_t[:])
                link(nc.vector.scalar_tensor_tensor(out=r_t[:], in0=r_oh[:], scalar=-2.0, in1=r_sc[:],
                                                    op0=ALU.mult, op1=ALU.add))
                first_of_the_greatest(r_t[:], r_oh2[:], r_t[:])
                link(nc.vector.tensor_tensor(r_oh[:], r_oh[:], r_oh2[:], ALU.add))
                link(nc.vector.tensor_tensor(comb[:, 0:EXPERTS, bass.ds(b * TT, TT)].rearrange("p e t -> p t e"),
                                             r_sc[:], r_oh[:], ALU.mult))
                assert count[0] == ROUTER_LINKS, count

            with dve.Fori(0, BATCHES) as b:
                normalise(b, 0)
                rope(b, 0)
                for r in range(STEPS + 1):
                    if r >= 1:
                        divide(b, r - 1)
                    if r < STEPS:
                        mask_and_max(b, r)
                    if r % TT == 2 and r // TT + 1 < GROUPS:
                        rope(b, r // TT + 1)
                add_to_residual(b, proj_mm, proj_added)
                for t in range(TT):
                    dve.wait_ge(e_mm, b * TT + t + 1)
                    nc.vector.tensor_reduce(mx[:, 0, t:t + 1], ps[:, t, :], AX_X, ALU.max).then_inc(e_max, 1)
                    dve.wait_ge(e_max, b * TT + t + 1)
                    nc.vector.tensor_scalar(nb[:, 0, t:t + 1], mx[:, 0, t:t + 1], -1.0, None, ALU.mult)\
                        .then_inc(e_nb, 1)
                normalise(b, 1)
                dve.wait_ge(e_exp, b * TT + TT)
                nc.vector.reciprocal(rsum[:, 0, :], sums[:, 0, :]).then_inc(e_rsum, 1)
                dve.wait_ge(e_rsum, b + 1)
                for t in range(TT):
                    nc.vector.tensor_scalar(probs[:, 0, t, :], probs[:, 0, t, :], rsum[:, 0, t:t + 1], None,
                                            ALU.mult).then_inc(a_ready, 1)
                add_to_residual(b, xm_mm, xm_added)
                normalise(b, 2)
                route(b)

            NF = len(HCHUNKS)
            for k in range(2):
                dve.nop().then_inc(e_used[k], 1)
            dve.nop().then_inc(h_done, 2)
            dve.nop().then_inc(y_added, 4)
            with dve.Fori(0, SLOTS // 2) as pair:
                for n in range(2 * BATCHES + 1):
                    if n < 2 * BATCHES:
                        for f, (f0, fn) in enumerate(HCHUNKS):
                            q = n * NF + f
                            dve.wait_ge(sg_done, pair * (2 * BATCHES * NF) + q + 1)
                            nc.vector.tensor_tensor(hT[n % 2][0:fn, f, :], sg[q % 2][0:fn, :],
                                                    ps[0:fn, 2 * (q % 2) + 1, :], ALU.mult).then_inc(h_done, 1)
                    if n >= 1:
                        k, tg = divmod(n - 1, BATCHES)
                        for t in range(TT):
                            tile = tg * TT + t
                            dve.wait_ge(y_mm, pair * (2 * TILES) + (n - 1) * TT + t + 1)
                            nc.vector.scalar_tensor_tensor(
                                out=acc[:, tile, :], in0=ps[:, 4 + t, :],
                                scalar=comb[:, bass.ds(pair * 2 + k, 1), tile:tile + 1].rearrange("p o t -> p (o t)"),
                                in1=acc[:, tile, :], op0=ALU.mult, op1=ALU.add).then_inc(y_added, 1)
                        if tg == BATCHES - 1:
                            dve.nop().then_inc(e_used[k], 1)


def rope_tables():
    theta = (1.0 / np.float32(10000.0) ** (np.arange(0, HDIM, 2, dtype=np.float32) / np.float32(HDIM))).astype(np.float32)
    angle = np.outer(np.arange(TOKENS, dtype=np.float32), theta).astype(np.float32)
    by_feature = np.repeat(np.arange(HDIM // 2), 2)
    sign = np.tile(np.array([-1.0, 1.0], np.float32), HDIM // 2)
    cos = np.cos(angle)[:, by_feature].T
    sin = (np.sin(angle)[:, by_feature] * sign).T
    return (np.ascontiguousarray(np.tile(cos, (GH, 1)), np.float32),
            np.ascontiguousarray(np.tile(sin, (GH, 1)), np.float32))


def kernel(**inputs):
    import concourse.bacc as _bacc
    from concourse.bass_utils import run_bass_kernel_spmd as _run

    i = {k: np.asarray(v) for k, v in inputs.items()}
    cos, sin = rope_tables()

    def halves(w, axis):
        return np.stack(np.split(w, SHARED, axis=axis))

    arrays = {
        "x": i["x"].reshape(BATCHES * TOKENS, DIM),
        "ctxT": i["ctx_1024"].transpose(0, 2, 1),
        "waT": i["L0_attn_w_atten"].T, "wpT": i["L0_attn_w_proj"].T,
        "wqT": i["L0_xattn_Wq"].T, "wkT": i["L0_xattn_Wk"].T,
        "bq": i["L0_xattn_bq"].reshape(P, 1), "bk": i["L0_xattn_bk"].reshape(P, 1),
        "wr": i["L0_ffn_W_router"],
        "wg": np.concatenate([i["L0_ffn_We_gate"], halves(i["L0_ffn_Ws_gate"], 1)]).reshape(SLOTS * DIM, EDIM),
        "wu": np.concatenate([i["L0_ffn_We_up"], halves(i["L0_ffn_Ws_up"], 1)]).reshape(SLOTS * DIM, EDIM),
        "wd": np.concatenate([i["L0_ffn_We_down"], halves(i["L0_ffn_Ws_down"], 0)]).reshape(SLOTS * EDIM, DIM),
        "cosT": cos, "sinT": sin,
    }
    arrays = {f"in_{k}": np.ascontiguousarray(v) for k, v in arrays.items()}
    nc = _bacc.Bacc("TRN2", target_bir_lowering=False, num_devices=1)
    args = [nc.dram_tensor(k, v.shape, mybir.dt.from_np(v.dtype), kind="ExternalInput").ap() for k, v in arrays.items()]
    out = nc.dram_tensor("out", (BATCHES * TOKENS, DIM), F32, kind="ExternalOutput").ap()
    build(nc, *args, out)
    r = _run(nc, [arrays], core_ids=[0])
    return r.results[0]["out"].reshape(BATCHES, TOKENS, DIM)
```

```python
from contextlib import ExitStack

import numpy as np

import concourse.bass as bass
from concourse import mybir

P = 128
F32 = mybir.dt.float32
F32R = mybir.dt.float32r
I32 = mybir.dt.int32
ALU = mybir.AluOpType
ACT = mybir.ActivationFunctionType
AX_X = mybir.AxisListType.X

BATCHES, TOKENS, DIM = 4, 512, 512
CTX = 256
HEADS, HDIM = 16, 32
EXPERTS, EDIM = 8, 352
SHARED = 2
SLOTS = EXPERTS + SHARED
TT = TOKENS // P
TILES = BATCHES * TT
CC = DIM // P
GROUPS = HEADS * HDIM // P
GH = P // HDIM
STEPS = GROUPS * TT
BT = 256
BA = BT // P
BLOCKS = BATCHES * TOKENS // BT
ROUTED_BLOCKS = 2 * BLOCKS + EXPERTS - 1
SLOT_COLS = (ROUTED_BLOCKS + 1) * BA
GU_SIZE, D_SIZE = SLOTS * 2 * DIM * EDIM, SLOTS * EDIM * DIM
PIECE = 704
PIECES = (GU_SIZE + D_SIZE) // (P * PIECE)
LATER_PIECES = (12, 2)
FIRST_PIECES = PIECES - (BATCHES - 1) * sum(LATER_PIECES)
EXP_LAG, DIVIDE_LAG, TURN_LAG, WEIGH_LAG = 1, 2, 3, 4
HCHUNKS = [(f * P, min(P, EDIM - f * P)) for f in range((EDIM + P - 1) // P)]
EPS = 1e-5
SCALE = float(HDIM) ** -0.5
MASKED = -1e30
LOWEST = -3e38


def build(nc, x, ctxT, waT, wpT, wqT, wkT, bq, bk, wr, we, cosT, sinT, out):
    with ExitStack() as stack:
        def sb(name, shape, dt=F32):
            return stack.enter_context(nc.sbuf_tensor(name, shape, dt))

        def sem(name):
            return stack.enter_context(nc.semaphore(name))

        acc = sb("acc", [P, TILES, DIM])
        ident = sb("ident", [P, P])
        onehot = sb("onehot", [P, 2, TILES, EXPERTS])
        weight = sb("weight", [P, 2, TILES])
        slot_i = sb("slot_i", [P, 2, TILES], I32)
        first_i = sb("first_i", [P, EXPERTS + 1], I32)
        xn3_d = nc.dram_tensor("xn3_d", [BATCHES * TOKENS, DIM], F32).ap()
        hi_d = nc.dram_tensor("hi_d", [GU_SIZE + D_SIZE], F32).ap()
        lo_d = nc.dram_tensor("lo_d", [GU_SIZE + D_SIZE], F32).ap()
        token_d = nc.dram_tensor("token_d", [SLOT_COLS * P, 1], I32).ap()
        y_d = nc.dram_tensor("y_d", [(ROUTED_BLOCKS + 1) * BT, DIM], F32).ap()

        attention = stack.enter_context(ExitStack())

        def sb(name, shape, dt=F32):
            return attention.enter_context(nc.sbuf_tensor(name, shape, dt))

        ctx_sb = sb("ctx_sb", [P, CTX // P, TOKENS])
        wa_sb = sb("wa_sb", [P, CC, 3 * DIM])
        wp_sb = sb("wp_sb", [P, CC, DIM])
        wq_sb = sb("wq_sb", [P, CTX // P, P])
        wk_sb = sb("wk_sb", [P, CTX // P, P])
        wr_sb = sb("wr_sb", [P, CC, EXPERTS])
        bias_sb = sb("bias_sb", [P, 2])
        cos_sb = sb("cos_sb", [P, TOKENS])
        sin_sb = sb("sin_sb", [P, TOKENS])
        mask = sb("mask", [P, TOKENS])
        iota8 = sb("iota8", [P, TT, EXPERTS])
        stats = sb("stats", [P, TT, 6])
        mv = sb("mv", [P, TT, 2])
        veps = sb("veps", [P, TT])
        rstd = sb("rstd", [P, TT])
        power = sb("power", [P, TT])
        xn = sb("xn", [P, TT, DIM])
        xnT = sb("xnT", [P, CC, TOKENS])
        v_sb = sb("v_sb", [P, TT, DIM])
        qz = sb("qz", [P, 2, GH, TOKENS])
        kr = sb("kr", [P, 2, TOKENS])
        rope_sw = sb("rope_sw", [P, TOKENS])
        rope_c = sb("rope_c", [P, TOKENS])
        assert WEIGH_LAG == TT
        probs = [sb(f"probs{i}", [P, GH, (i + 1) * P]) for i in range(TT)]
        probsT = sb("probsT", [P, 2, GH, TOKENS])
        mx = sb("mx", [P, 2, GH])
        nb = sb("nb", [P, 2, GH])
        sums = sb("sums", [P, 2, GH])
        rsum = sb("rsum", [P, 2, GH])
        yT = sb("yT", [P, GROUPS, TOKENS])
        q2 = sb("q2", [P, TOKENS])
        k2 = sb("k2", [P, TOKENS])
        xn_xT = sb("xn_xT", [P, CC, TOKENS])
        att = sb("att", [P, 2, TOKENS])
        attT = sb("attT", [P, TT, TOKENS])
        a_mx = sb("a_mx", [P, TT])
        a_nb = sb("a_nb", [P, TT])
        a_sums = sb("a_sums", [P, TT])
        a_rsum = sb("a_rsum", [P, TT])
        r_sc = sb("r_sc", [P, TT, EXPERTS])
        r_t = sb("r_t", [P, TT, EXPERTS])
        r_m = sb("r_m", [P, TT])
        r_oh = sb("r_oh", [P, TT, EXPERTS])
        piece_raw = sb("piece_raw", [P, PIECE])
        piece_hi = sb("piece_hi", [P, PIECE])
        attention.close()

        def sb(name, shape, dt=F32):
            return stack.enter_context(nc.sbuf_tensor(name, shape, dt))

        gu_hi = [sb(f"gu_hi{k}", [P, 2 * CC, EDIM], F32R) for k in range(2)]
        gu_lo = [sb(f"gu_lo{k}", [P, 2 * CC, EDIM], F32R) for k in range(2)]
        d_hi = [sb(f"d_hi{k}", [P, len(HCHUNKS), DIM], F32R) for k in range(2)]
        d_lo = [sb(f"d_lo{k}", [P, len(HCHUNKS), DIM], F32R) for k in range(2)]
        sg = sb("sg", [P, len(HCHUNKS), BT])
        hf = sb("hf", [P, len(HCHUNKS), BT])
        h_hi = sb("h_hi", [P, len(HCHUNKS), BT], F32R)
        h_lo = sb("h_lo", [P, len(HCHUNKS), BT], F32R)
        y_sb = sb("y_sb", [P, BA, DIM])
        picked = sb("picked", [P, 2, 2, DIM])
        pick_i = sb("pick_i", [P, 2, 2], I32)
        tri = sb("tri", [P, P])
        ones = sb("ones", [P, P])
        zero_row = sb("zero_row", [P, DIM])
        tok_i = sb("tok_i", [P, TILES], I32)
        table_zero = sb("table_zero", [P, SLOT_COLS], I32)
        table = sb("table", [P, SLOT_COLS], I32)
        table_cur = sb("table_cur", [P, BA], I32)
        both = sb("both", [P, TILES, EXPERTS])
        tots = sb("tots", [P, TILES, EXPERTS])
        before = sb("before", [P, TILES + 1, EXPERTS])
        steps = sb("steps", [P, EXPERTS, BLOCKS - 1])
        more = sb("more", [P, EXPERTS, BLOCKS - 1])
        nblk = sb("nblk", [P, EXPERTS])
        first = sb("first", [P, EXPERTS + 1])
        first_row = sb("first_row", [P, EXPERTS])
        row = sb("row", [P, TILES, EXPERTS])
        row_k = sb("row_k", [P, 2, TILES])
        place_lo = sb("place_lo", [P, 2, TILES], I32)
        place_hi = sb("place_hi", [P, 2, TILES], I32)
        place_i = sb("place_i", [P, 2, TILES], I32)

        class Path:
            def __init__(self, name):
                self.x = sb(name + "_x", [P, BA, DIM])
                self.xT_hi = sb(name + "_xT_hi", [P, CC, BT], F32R)
                self.xT_lo = sb(name + "_xT_lo", [P, CC, BT], F32R)
                self.x_loaded = sem(name + "_x_loaded")
                self.x_turned = sem(name + "_x_turned")
                self.xT_hi_done = sem(name + "_xT_hi_done")
                self.xT_done = sem(name + "_xT_done")
                self.gu_mm = sem(name + "_gu_mm")
                self.sg_done = sem(name + "_sg_done")
                self.h_done = sem(name + "_h_done")
                self.h_hi_done = sem(name + "_h_hi_done")
                self.hT_done = sem(name + "_hT_done")
                self.y_mm = sem(name + "_y_mm")
                self.y_out = sem(name + "_y_out")

        shared, routed = Path("shared"), Path("routed")
        shared.loads, routed.loads = 1, BA

        ps = stack.enter_context(nc.psum_tensor("ps", [P, 8, 512], F32))
        S_BANK, T_BANK, O_BANK, QK_BANK, X_BANK = 0, 2, 4, 5, 6
        ENERGIES = {1: (0, 1), 3: (2, 3)}
        TURNS = {2: (0, 1), 4: (2, 3)}
        LN2_TURNS = {5: (0, 1), 6: (2, 3)}
        MIXES = {7: (0,), 8: (1,), 9: (2,), 10: (3,)}
        LN3_TURNS = {12: (0, 1), 13: (2, 3)}
        ROUTE = 14

        x_loaded = sem("x_loaded")
        w_loaded = sem("w_loaded")
        ctx_loaded = sem("ctx_loaded")
        ctx_used = sem("ctx_used")
        consts = sem("consts")
        zeroed = sem("zeroed")
        ln_stats = sem("ln_stats")
        ln_var = sem("ln_var")
        ln_rstd = sem("ln_rstd")
        ln_xn = sem("ln_xn")
        ln_tr = sem("ln_tr")
        ln_xnT = sem("ln_xnT")
        v_mm = sem("v_mm")
        v_done = sem("v_done")
        qk_mm = sem("qk_mm")
        qk_used = sem("qk_used")
        rope_link = sem("rope_link")
        rope_done = sem("rope_done")
        s_mm = sem("s_mm")
        s_masked = sem("s_masked")
        nb_done = sem("nb_done")
        exp_done = sem("exp_done")
        rsum_done = sem("rsum_done")
        p_ready = sem("p_ready")
        pT_mm = sem("pT_mm")
        pT_done = sem("pT_done")
        pv_mm = sem("pv_mm")
        yT_done = sem("yT_done")
        proj_mm = sem("proj_mm")
        proj_added = sem("proj_added")
        qk2_mm = sem("qk2_mm")
        qk2_done = sem("qk2_done")
        e_mm = sem("e_mm")
        e_max = sem("e_max")
        e_nb = sem("e_nb")
        e_exp = sem("e_exp")
        e_rsum = sem("e_rsum")
        a_ready = sem("a_ready")
        aT_mm = sem("aT_mm")
        aT_done = sem("aT_done")
        xm_mm = sem("xm_mm")
        xm_added = sem("xm_added")
        xn3_stored = sem("xn3_stored")
        piece_loaded = sem("piece_loaded")
        piece_split = sem("piece_split")
        piece_stored = sem("piece_stored")
        r_mm = sem("r_mm")
        r_link = sem("r_link")
        r_shift = sem("r_shift")
        r_exp = sem("r_exp")
        e_loaded = [sem("e_loaded0"), sem("e_loaded1")]
        e_used = [sem("e_used0"), sem("e_used1")]
        first_cast = sem("first_cast")
        later_cast = sem("later_cast")
        consts_b = sem("consts_b")
        both_done = sem("both_done")
        count_mm = sem("count_mm")
        d_link = sem("d_link")
        slots_ready = sem("slots_ready")
        table_cleared = sem("table_cleared")
        table_written = sem("table_written")
        table_loaded = sem("table_loaded")
        cur_copied = sem("cur_copied")
        y_stored = sem("y_stored")
        pick_copied = sem("pick_copied")
        pick_loaded = [sem("pick_loaded0"), sem("pick_loaded1")]
        picked_used = [sem("picked_used0"), sem("picked_used1")]
        acc_link = sem("acc_link")
        tile_done = sem("tile_done")
        stored = sem("stored")

        waited = sem("waited")

        def pass_wait(eng):
            eng.nop().then_inc(waited, 1)

        W_LOADS = 10
        ROUTER_LINKS = 19
        NF = len(HCHUNKS)
        NX = 6 * 16

        def load_expert(sp, s, buf, uses):
            sp.wait_ge(e_used[buf], uses)
            for gu_dst, d_dst, parts in ((gu_hi[buf], d_hi[buf], hi_d), (gu_lo[buf], d_lo[buf], lo_d)):
                gu = parts[0:GU_SIZE].rearrange("(r p n) -> p r n", p=P, n=EDIM)
                d = parts[GU_SIZE:GU_SIZE + D_SIZE].rearrange("(r n) -> r n", n=DIM)
                sp.dma_start(gu_dst[:].bitcast(F32), gu[:, bass.ds(s * (2 * CC), 2 * CC), :]).then_inc(e_loaded[buf], 16)
                sp.dma_start(d_dst[:, 0:NF - 1, :].bitcast(F32), d[bass.ds(s * EDIM, (NF - 1) * P), :]
                             .rearrange("(f p) n -> p f n", p=P)).then_inc(e_loaded[buf], 16)
                f0, fn = HCHUNKS[-1]
                sp.dma_start(d_dst[0:fn, NF - 1, :].bitcast(F32), d[bass.ds(s * EDIM + f0, fn), :])\
                    .then_inc(e_loaded[buf], 16)

        def block_range(eng, e):
            lo = eng.value_load(first_i[0:1, bass.ds(e, 1)], min_val=0, max_val=ROUTED_BLOCKS - 1)
            hi = eng.value_load(first_i[0:1, bass.ds(e + 1, 1)], min_val=1, max_val=ROUTED_BLOCKS)
            return lo, hi

        x_v = x.rearrange("(b t p) d -> b p t d", p=P, t=TT)
        out_v = out.rearrange("(t p) d -> p t d", p=P)
        xn3_v = xn3_d.rearrange("(t p) d -> p t d", p=P)

        we_p, hi_p, lo_p = (w.rearrange("(i p n) -> p i n", p=P, n=PIECE) for w in (we, hi_d, lo_d))

        def split_range(eng, first, count, step):
            pass_wait(eng)
            with eng.Fori(0, count) as i:
                step(first + i)

        def later_piece(b, part):
            return b * sum(LATER_PIECES) + (FIRST_PIECES - sum(LATER_PIECES) + part * LATER_PIECES[0])

        ctx_v = ctxT.rearrange("b (c p) n -> p (b c) n", p=P)
        NCTX = CTX // P

        block = stack.enter_context(nc.Block())

        @block.sync
        def _(sp):
            sp.dma_start(acc[:, 0:TT, :], x_v[0]).then_inc(x_loaded, 16)
            loads = [(wa_sb[:], waT.rearrange("(c p) n -> p c n", p=P)), (cos_sb[:], cosT), (sin_sb[:], sinT),
                     (wp_sb[:], wpT.rearrange("(c p) n -> p c n", p=P)),
                     (wq_sb[:], wqT.rearrange("(c p) n -> p c n", p=P)),
                     (wk_sb[:], wkT.rearrange("(c p) n -> p c n", p=P)),
                     (wr_sb[:], wr.rearrange("(c p) n -> p c n", p=P)),
                     (bias_sb[:, 0:1], bq), (bias_sb[:, 1:2], bk)]
            for dst, src in loads:
                sp.dma_start(dst, src).then_inc(w_loaded, 16)
            sp.dma_start(acc[:, TT:TILES, :], x[TT * P:, :].rearrange("(t p) d -> p t d", p=P)).then_inc(w_loaded, 16)

            def load_context(p):
                sp.wait_ge(ctx_used, p + 1)
                sp.dma_start(ctx_sb[:], ctx_v[:, bass.ds(p * NCTX, NCTX), :]).then_inc(ctx_loaded, 16)

            def move_piece(n):
                sp.wait_ge(piece_stored, n * 16 + 16)
                at = bass.ds(n, 1)
                for dst, src in ((piece_raw, we_p), (piece_hi, hi_p)):
                    sp.dma_start(dst[:], src[:, at, :].rearrange("p o n -> p (o n)")).then_inc(piece_loaded, 16)
                sp.wait_ge(piece_split, n + 1)
                sp.dma_start(lo_p[:, at, :].rearrange("p o n -> p (o n)"), piece_raw[:]).then_inc(piece_stored, 16)

            def store_xn3(p, ln):
                sp.wait_ge(ln_xn, ln * TT + TT)
                sp.dma_start(xn3_v[:, bass.ds(p * TT, TT), :], xn[:]).then_inc(xn3_stored, 16)

            sp.nop().then_inc(piece_stored, 16)
            sp.wait_ge(first_cast, 16)
            split_range(sp, 0, FIRST_PIECES, move_piece)
            with sp.Fori(1, BATCHES) as b:
                load_context(b - 1)
                sp.wait_ge(later_cast, 16)
                split_range(sp, later_piece(b, 0), LATER_PIECES[0], move_piece)
                store_xn3(b - 1, b * 3)
                split_range(sp, later_piece(b, 1), LATER_PIECES[1], move_piece)
            load_context(BATCHES - 1)
            store_xn3(BATCHES - 1, BATCHES * 3 - 1)

            def load_tokens(block):
                sp.dma_start(shared.x[:], xn3_v[:, bass.ds(block * BA, BA), :]).then_inc(shared.x_loaded, 16)

            sp.wait_ge(r_link, BATCHES * ROUTER_LINKS)
            sp.wait_ge(xn3_stored, 16 * BATCHES + 1)
            sp.wait_ge(piece_stored, 16 * PIECES + 16)
            load_expert(sp, 0, 0, 1)
            load_tokens(0)
            load_expert(sp, 1, 1, 1)
            sp.wait_ge(consts_b, 6)
            sp.dma_start(token_d.rearrange("(p n) o -> p (n o)", p=P), table_zero[:]).then_inc(table_cleared, 16)
            with sp.Fori(0, BLOCKS) as j:
                sp.wait_ge(shared.x_turned, j * BA + BA)
                load_tokens((j + 1) % BLOCKS)
            sp.wait_ge(slots_ready, 1)
            with sp.Fori(0, EXPERTS // 2) as pair:
                for k in range(2):
                    e, buf = pair * 2 + k, k
                    load_expert(sp, e + 2, buf, pair + 2)
                    lo, hi = block_range(sp, e)
                    with sp.Fori(lo, hi) as j:
                        sp.wait_ge(routed.y_out, j * BA + (BA + 2))
                        sp.dma_start(y_d[bass.ds(j * BT, BT), :].rearrange("(a p) d -> p a d", p=P), y_sb[:])\
                            .then_inc(y_stored, 16)
            total = sp.value_load(first_i[0:1, EXPERTS:EXPERTS + 1], min_val=1, max_val=ROUTED_BLOCKS)
            with sp.Fori(total, ROUTED_BLOCKS + 1) as j:
                sp.dma_start(y_d[bass.ds(j * BT, BT), :].rearrange("(a p) d -> p a d", p=P),
                             zero_row[:].unsqueeze(1).to_broadcast([P, BA, DIM])).then_inc(y_stored, 16)
            with sp.Fori(0, BLOCKS) as j:
                sp.wait_ge(shared.x_turned, j * BA + (BLOCKS + 1) * BA)
                load_tokens((j + 1) % BLOCKS)
                sp.wait_ge(tile_done, j + 1)
                sp.dma_start(out_v[:, bass.ds(j * BA, BA), :], acc[:, bass.ds(j * BA, BA), :]).then_inc(stored, 16)
            sp.wait_ge(stored, 16 * BLOCKS)

        @block.gpsimd
        def _(pool):
            nc.gpsimd.memset(ident[:], 0.0).then_inc(zeroed, 1)
            nc.gpsimd.memset(mask[:], 0.0).then_inc(zeroed, 1)
            nc.gpsimd.memset(power[:], -0.5).then_inc(zeroed, 1)
            pool.wait_ge(zeroed, 3)
            nc.gpsimd.affine_select(out=ident[:], in_=ident[:], compare_op=ALU.not_equal, fill=1.0, base=0,
                                    pattern=[[-1, P]], channel_multiplier=1).then_inc(consts, 1)
            diag = mask[:, TOKENS - P:TOKENS]
            nc.gpsimd.affine_select(out=diag, in_=diag, compare_op=ALU.is_ge, fill=MASKED, base=0,
                                    pattern=[[-1, P]], channel_multiplier=1).then_inc(consts, 1)
            nc.gpsimd.iota(iota8[:], pattern=[[0, TT], [1, EXPERTS]], base=0, channel_multiplier=0,
                           allow_small_or_imprecise_dtypes=True).then_inc(consts, 1)

            def root(ln):
                pool.wait_ge(ln_var, ln + 1)
                nc.gpsimd.tensor_tensor(rstd[:], veps[:], power[:], ALU.pow).then_inc(ln_rstd, 1)

            def cast(first, count, done):
                at = bass.ds(first * (P * PIECE), count * (P * PIECE))
                pool.dma_start(hi_d[at].bitcast(F32R).rearrange("(r n) -> r n", n=PIECE),
                               we[at].rearrange("(r n) -> r n", n=PIECE)).then_inc(done, 16)

            def take_off(n):
                pool.wait_ge(piece_loaded, n * 32 + 32)
                nc.gpsimd.tensor_tensor(piece_raw[:].bitcast(F32R), piece_raw[:], piece_hi[:], ALU.subtract)\
                    .then_inc(piece_split, 1)

            pool.wait_ge(w_loaded, 16 * W_LOADS)
            cast(0, FIRST_PIECES, first_cast)
            root(0)
            cast(FIRST_PIECES, PIECES - FIRST_PIECES, later_cast)
            split_range(pool, 0, FIRST_PIECES, take_off)
            with pool.Fori(1, BATCHES) as b:
                root(b * 3 - 2)
                root(b * 3 - 1)
                pass_wait(pool)
                split_range(pool, later_piece(b, 0), LATER_PIECES[0], take_off)
                root(b * 3)
                split_range(pool, later_piece(b, 1), LATER_PIECES[1], take_off)
            root(BATCHES * 3 - 2)
            root(BATCHES * 3 - 1)
            pool.wait_ge(r_link, BATCHES * ROUTER_LINKS)
            pool.wait_ge(xn3_stored, 16 * BATCHES + 1)
            nc.gpsimd.memset(table_zero[:], 0).then_inc(consts_b, 1)
            nc.gpsimd.memset(tri[:], 1.0).then_inc(zeroed, 1)
            nc.gpsimd.memset(ones[:], 1.0).then_inc(consts_b, 1)
            nc.gpsimd.memset(zero_row[:], 0.0).then_inc(consts_b, 1)
            nc.gpsimd.iota(tok_i[:], pattern=[[P, TILES]], base=0, channel_multiplier=1).then_inc(consts_b, 1)
            nc.gpsimd.iota(steps[:], pattern=[[0, EXPERTS], [BT, BLOCKS - 1]], base=BT, channel_multiplier=0,
                           allow_small_or_imprecise_dtypes=True).then_inc(consts_b, 1)
            pool.wait_ge(zeroed, 4)
            nc.gpsimd.affine_select(out=tri[:], in_=tri[:], compare_op=ALU.is_ge, fill=0.0, base=-1,
                                    pattern=[[1, P]], channel_multiplier=-1).then_inc(consts_b, 1)
            pool.wait_ge(slots_ready, 1)
            pool.wait_ge(table_cleared, 16)
            for k in range(2):
                for t in range(TILES):
                    pool.indirect_dma_start(out=token_d, out_offset=bass.IndirectOffsetOnAxis(
                        ap=place_i[:, k, t:t + 1], axis=0), in_=tok_i[:, t:t + 1], in_offset=None)\
                        .then_inc(table_written, 16)
            pool.wait_ge(table_written, 16 * 2 * TILES)
            pool.dma_start(table[:], token_d.rearrange("(p n) o -> p (n o)", p=P)).then_inc(table_loaded, 16)
            pool.wait_ge(table_loaded, 16)

            def gather(block):
                nc.gpsimd.tensor_copy(table_cur[:], table[:, bass.ds(block * BA, BA)]).then_inc(cur_copied, 1)
                pool.wait_ge(cur_copied, block + 1)
                pass_wait(pool)
                for a in range(BA):
                    pool.indirect_dma_start(out=routed.x[:, a, :], out_offset=None, in_=xn3_d,
                                            in_offset=bass.IndirectOffsetOnAxis(ap=table_cur[:, a:a + 1], axis=0))\
                        .then_inc(routed.x_loaded, 16)

            gather(0)
            with pool.Fori(0, EXPERTS // 2) as pair:
                for k in range(2):
                    e = pair * 2 + k
                    lo, hi = block_range(pool, e)
                    with pool.Fori(lo, hi) as j:
                        pool.wait_ge(routed.x_turned, j * BA + BA)
                        pass_wait(pool)
                        gather(j + 1)
            pool.wait_ge(y_stored, (ROUTED_BLOCKS + 1) * 16 + 16)
            with pool.Fori(0, BLOCKS) as j:
                pool.wait_ge(picked_used[0], j + 1)
                pool.wait_ge(picked_used[1], j + 1)
                pass_wait(pool)
                nc.gpsimd.tensor_copy(pick_i[:], slot_i[:, :, bass.ds(j * BA, BA)]).then_inc(pick_copied, 1)
                pool.wait_ge(pick_copied, j + 1)
                pass_wait(pool)
                for a in range(BA):
                    for k in range(2):
                        pool.indirect_dma_start(out=picked[:, a, k, :], out_offset=None, in_=y_d,
                                                in_offset=bass.IndirectOffsetOnAxis(ap=pick_i[:, k, a:a + 1], axis=0))\
                            .then_inc(pick_loaded[a], 16)

        @block.scalar
        def _(act):
            act.wait_ge(w_loaded, 16 * W_LOADS)

            def copy_turned(dst, ln, tiles):
                for t in tiles:
                    act.wait_ge(ln_tr, ln * TT + t + 1)
                    nc.scalar.copy(dst[:, :, t * P:(t + 1) * P],
                                   ps[:, X_BANK + t % 2, :].rearrange("p (c n) -> p c n", c=CC)).then_inc(ln_xnT, 1)

            def exponentials(b, n, h):
                w = (n % TT + 1) * P
                if h == 0:
                    act.wait_ge(nb_done, b * STEPS + n + 1)
                pr = probs[n % TT][:, h, 0:w]
                nc.scalar.activation(pr, pr, ACT.Exp, bias=nb[:, n % 2, h:h + 1], scale=SCALE,
                                     accum_out=sums[:, n % 2, h:h + 1]).then_inc(exp_done, 1)

            def copy_probsT(b, n, h):
                w = (n % TT + 1) * P
                if n >= 2 and h == 0:
                    act.wait_ge(pv_mm, b * STEPS + n - 1)
                act.wait_ge(pT_mm, b * HEADS * TT + GH * n + h + 1)
                nc.scalar.copy(probsT[:, n % 2, h, 0:w], ps[:, T_BANK + h % 2, 0:w]).then_inc(pT_done, 1)

            def copy_yT(b, n):
                if n % TT == TT - 1:
                    act.wait_ge(pv_mm, b * STEPS + n + 1)
                    nc.scalar.copy(yT[:, n // TT, :], ps[:, O_BANK, :]).then_inc(yT_done, 1)

            def cross(p, ln, r):
                if r == 0:
                    for i, dst in enumerate((q2, k2)):
                        act.wait_ge(qk2_mm, p * 2 + i + 1)
                        nc.scalar.activation(dst[:], ps[:, X_BANK + i, :], ACT.Identity, bias=bias_sb[:, i:i + 1],
                                             scale=1.0).then_inc(qk2_done, 1)
                if r in ENERGIES:
                    for t in ENERGIES[r]:
                        act.wait_ge(e_nb, p * TT + t + 1)
                        nc.scalar.activation(att[:, t % 2, :], ps[:, X_BANK + t % 2, :], ACT.Exp, bias=a_nb[:, t:t + 1],
                                             scale=1.0, accum_out=a_sums[:, t:t + 1]).then_inc(e_exp, 1)
                if r in TURNS:
                    for t in TURNS[r]:
                        act.wait_ge(aT_mm, p * TT + t + 1)
                        nc.scalar.copy(attT[:, :, t * P:(t + 1) * P],
                                       ps[:, X_BANK + t % 2, :].rearrange("p (c n) -> p c n", c=TT)).then_inc(aT_done, 1)
                if r in LN2_TURNS:
                    copy_turned(xn_xT, ln, LN2_TURNS[r])
                if r in LN3_TURNS:
                    copy_turned(xn_xT, ln + 1, LN3_TURNS[r])
                if r == ROUTE:
                    act.wait_ge(r_shift, p + 2)
                    nc.scalar.activation(r_sc[:], r_t[:], ACT.Exp).then_inc(r_exp, 1)

            def attend(b, ln, p):
                copy_turned(xnT, ln, range(TT))
                for t in range(TT):
                    act.wait_ge(v_mm, b * TT + t + 1)
                    nc.scalar.copy(v_sb[:, t, :], ps[:, X_BANK + t % 2, :]).then_inc(v_done, 1)
                for r in range(STEPS + WEIGH_LAG):
                    for h in range(GH):
                        if 0 <= r - EXP_LAG < STEPS:
                            exponentials(b, r - EXP_LAG, h)
                        if 0 <= r - TURN_LAG < STEPS:
                            copy_probsT(b, r - TURN_LAG, h)
                    if 0 <= r - WEIGH_LAG < STEPS:
                        copy_yT(b, r - WEIGH_LAG)
                    if p is not None:
                        cross(p, ln + 1, r)

            attend(0, 0, None)
            with act.Fori(1, BATCHES) as b:
                attend(b, b * 3 - 2, b - 1)
            for r in range(ROUTE + 1):
                cross(BATCHES - 1, 3 * BATCHES - 2, r)

            def turn(path, block):
                for a in range(BA):
                    act.wait_ge(path.x_turned, block * BA + a + 1)
                    nc.scalar.copy(path.xT_hi[:, :, a * P:(a + 1) * P],
                                   ps[:, 3 + a, :].rearrange("p (c n) -> p c n", c=CC)).then_inc(path.xT_hi_done, 1)

            def silu(path, j):
                for f in range(NF + 1):
                    if f < NF:
                        fn = HCHUNKS[f][1]
                        act.wait_ge(path.gu_mm, j * NF + f + 1)
                        nc.scalar.activation(sg[0:fn, f, :], ps[0:fn, f, 0:BT], ACT.Silu).then_inc(path.sg_done, 1)
                    if f >= 1:
                        fn = HCHUNKS[f - 1][1]
                        act.wait_ge(path.h_done, j * NF + NF + f)
                        nc.scalar.copy(h_hi[0:fn, f - 1, :], hf[0:fn, f - 1, :]).then_inc(path.h_hi_done, 1)
                turn(path, j + 1)

            turn(shared, 0)
            with act.Fori(0, BLOCKS) as j:
                silu(shared, j)
            turn(routed, 0)
            act.wait_ge(slots_ready, 1)
            with act.Fori(0, EXPERTS) as e:
                lo, hi = block_range(act, e)
                with act.Fori(lo, hi) as j:
                    silu(routed, j)
            with act.Fori(BLOCKS, 2 * BLOCKS) as j:
                silu(shared, j)

        @block.tensor
        def _(pe):
            pe.nop().then_inc(ctx_used, 1)
            pe.wait_ge(consts, 3)
            pe.wait_ge(w_loaded, 16 * W_LOADS)

            def turn_ln(ln, tiles, free):
                for t in tiles:
                    pe.wait_ge(ln_xn, ln * TT + t + 1)
                    if t < 2:
                        pe.wait_ge(free[t][0], free[t][1])
                    else:
                        pe.wait_ge(ln_xnT, ln * TT + t - 1)
                    for c in range(CC):
                        last = nc.tensor.transpose(ps[:, X_BANK + t % 2, c * P:(c + 1) * P], xn[:, t, c * P:(c + 1) * P],
                                                   ident[:])
                    last.then_inc(ln_tr, 1)

            def project_qk(b, g):
                for i in range(2):
                    e = 2 * g + i
                    if e >= 1:
                        pe.wait_ge(qk_used, b * 2 * GROUPS + e)
                    for c in range(CC):
                        col = i * DIM + g * P
                        last = nc.tensor.matmul(ps[:, QK_BANK, :], wa_sb[:, c, col:col + P], xnT[:, c, :],
                                                start=(c == 0), stop=(c == CC - 1))
                    last.then_inc(qk_mm, 1)

            def scores(b, n, h):
                g, i = divmod(n, TT)
                w = (i + 1) * P
                if h == 0:
                    pe.wait_ge(rope_done, b * 2 * GROUPS + 2 * g + 2)
                if n or h >= 2:
                    pe.wait_ge(s_masked, b * HEADS * TT + GH * n + h - 1)
                nc.tensor.matmul(ps[:, S_BANK + h % 2, 0:w], qz[:, g % 2, h, i * P:(i + 1) * P], kr[:, g % 2, 0:w],
                                 start=True, stop=True).then_inc(s_mm, 1)

            def turn_probs(b, n, h):
                pe.wait_ge(p_ready, b * HEADS * TT + GH * n + h + 1)
                if n or h >= 2:
                    pe.wait_ge(pT_done, b * HEADS * TT + GH * n + h - 1)
                for j in range(n % TT + 1):
                    last = nc.tensor.transpose(ps[:, T_BANK + h % 2, j * P:(j + 1) * P],
                                               probs[n % TT][:, h, j * P:(j + 1) * P], ident[:])
                last.then_inc(pT_mm, 1)

            def weigh(b, n, j):
                g, i = divmod(n, TT)
                if j == 0:
                    pe.wait_ge(pT_done, b * HEADS * TT + GH * n + GH)
                    if i == 0 and g >= 1:
                        pe.wait_ge(yT_done, b * GROUPS + g)
                for h in range(GH):
                    last = nc.tensor.matmul(ps[h * HDIM:(h + 1) * HDIM, O_BANK, i * P:(i + 1) * P],
                                            v_sb[:, j, g * P + h * HDIM:g * P + (h + 1) * HDIM],
                                            probsT[:, n % 2, h, j * P:(j + 1) * P],
                                            start=(j == 0), stop=(j == i), skip_group_check=True)
                if j == i:
                    last.then_inc(pv_mm, 1)

            def project_out(p):
                pe.wait_ge(yT_done, p * GROUPS + GROUPS)
                pe.wait_ge(r_shift, p + 1)
                for t in range(TT):
                    if t >= 2:
                        pe.wait_ge(proj_added, p * TT + t - 1)
                    for c in range(CC):
                        last = nc.tensor.matmul(ps[:, X_BANK + t % 2, :], yT[:, c, t * P:(t + 1) * P], wp_sb[:, c, :],
                                                start=(c == 0), stop=(c == CC - 1))
                    last.then_inc(proj_mm, 1)

            def cross(p, ln, r, free=None):
                if r == 0:
                    pe.wait_ge(ctx_loaded, p * 16 + 16)
                    pe.wait_ge(free[0], free[1])
                    for i, w in enumerate((wq_sb, wk_sb)):
                        for c in range(NCTX):
                            last = nc.tensor.matmul(ps[:, X_BANK + i, :], w[:, c, :], ctx_sb[:, c, :],
                                                    start=(c == 0), stop=(c == NCTX - 1))
                        last.then_inc(qk2_mm, 1)
                if r in ENERGIES:
                    for t in ENERGIES[r]:
                        if t < 2:
                            pe.wait_ge(qk2_done, p * 2 + 2)
                        else:
                            pe.wait_ge(aT_done, p * TT + t - 1)
                        nc.tensor.matmul(ps[:, X_BANK + t % 2, :], q2[:, t * P:(t + 1) * P], k2[:], start=True, stop=True)\
                            .then_inc(e_mm, 1)
                    if TT - 1 in ENERGIES[r]:
                        pe.nop().then_inc(ctx_used, 1)
                if r in TURNS:
                    for t in TURNS[r]:
                        pe.wait_ge(a_ready, p * TT + t + 1)
                        for c in range(TT):
                            last = nc.tensor.transpose(ps[:, X_BANK + t % 2, c * P:(c + 1) * P],
                                                       att[:, t % 2, c * P:(c + 1) * P], ident[:])
                        last.then_inc(aT_mm, 1)
                if r in LN2_TURNS:
                    turn_ln(ln, LN2_TURNS[r], [(aT_done, p * TT + TT - 1), (aT_done, p * TT + TT)])
                if r in MIXES:
                    for t in MIXES[r]:
                        if t < 2:
                            pe.wait_ge(aT_done, p * TT + TT)
                            pe.wait_ge(ln_xnT, ln * TT + TT)
                        else:
                            pe.wait_ge(xm_added, p * TT + t - 1)
                        for c in range(TT):
                            last = nc.tensor.matmul(ps[:, X_BANK + t % 2, :], xn_xT[:, c, t * P:(t + 1) * P], attT[:, c, :],
                                                    start=(c == 0), stop=(c == TT - 1))
                        last.then_inc(xm_mm, 1)
                if r in LN3_TURNS:
                    turn_ln(ln + 1, LN3_TURNS[r], [(xm_added, p * TT + TT - 1), (xm_added, p * TT + TT)])
                if r == ROUTE:
                    pe.wait_ge(ln_xnT, (ln + 1) * TT + TT)
                    for t in range(TT):
                        for c in range(CC):
                            last = nc.tensor.matmul(ps[:, X_BANK, t * EXPERTS:(t + 1) * EXPERTS],
                                                    xn_xT[:, c, t * P:(t + 1) * P], wr_sb[:, c, :],
                                                    start=(c == 0), stop=(c == CC - 1))
                    last.then_inc(r_mm, 1)

            def attend(b, ln, p):
                if p is None:
                    free = [(consts, 3), (consts, 3)]
                else:
                    project_out(p)
                    free = [(proj_added, p * TT + TT - 1), (proj_added, p * TT + TT)]
                turn_ln(ln, range(TT), free)
                for t in range(TT):
                    pe.wait_ge(ln_xnT, ln * TT + TT)
                    if t >= 2:
                        pe.wait_ge(v_done, b * TT + t - 1)
                    for c in range(CC):
                        last = nc.tensor.matmul(ps[:, X_BANK + t % 2, :], xnT[:, c, t * P:(t + 1) * P],
                                                wa_sb[:, c, 2 * DIM:3 * DIM], start=(c == 0), stop=(c == CC - 1))
                    last.then_inc(v_mm, 1)
                    if t == 1:
                        project_qk(b, 0)
                for r in range(STEPS + WEIGH_LAG):
                    for h in range(GH):
                        if r < STEPS:
                            scores(b, r, h)
                        if 0 <= r - WEIGH_LAG < STEPS and h <= (r - WEIGH_LAG) % TT:
                            weigh(b, r - WEIGH_LAG, h)
                        if 0 <= r - TURN_LAG < STEPS:
                            turn_probs(b, r - TURN_LAG, h)
                    if r % TT == 2 and r // TT + 1 < GROUPS:
                        project_qk(b, r // TT + 1)
                    if r == 0:
                        pe.wait_ge(v_done, b * TT + TT)
                    if p is not None:
                        cross(p, ln + 1, r, (v_done, b * TT + TT))

            attend(0, 0, None)
            with pe.Fori(1, BATCHES) as b:
                attend(b, b * 3 - 2, b - 1)
            project_out(BATCHES - 1)
            for r in range(ROUTE + 1):
                cross(BATCHES - 1, 3 * BATCHES - 2, r, (proj_added, BATCHES * TT))
            pe.wait_ge(r_shift, BATCHES + 1)

            def turn(path, block):
                pe.wait_ge(path.x_loaded, block * (16 * path.loads) + 16 * path.loads)
                for a in range(BA):
                    for c in range(CC):
                        last = nc.tensor.transpose(ps[:, 3 + a, c * P:(c + 1) * P], path.x[:, a, c * P:(c + 1) * P],
                                                   ident[:])
                    last.then_inc(path.x_turned, 1)

            def expert(path, j, buf):
                pe.wait_ge(path.xT_done, j * BA + BA)
                for f, (f0, fn) in enumerate(HCHUNKS):
                    pe.wait_ge(path.h_done, j * NF + f + 1)
                    for m in range(2):
                        terms = [(w, xT, m * CC + c, c) for w, xT in ((gu_hi[buf], path.xT_hi), (gu_lo[buf], path.xT_hi),
                                                                      (gu_hi[buf], path.xT_lo)) for c in range(CC)]
                        for i, (w, xT, r, c) in enumerate(terms):
                            last = nc.tensor.matmul(ps[0:fn, f, m * BT:(m + 1) * BT], w[:, r, f0:f0 + fn], xT[:, c, :],
                                                    start=(i == 0), stop=(i == len(terms) - 1))
                    last.then_inc(path.gu_mm, 1)
                turn(path, j + 1)
                pe.wait_ge(path.y_out, j * BA + BA)
                for f, (f0, fn) in enumerate(HCHUNKS):
                    pe.wait_ge(path.hT_done, j * NF + f + 1)
                    for a in range(BA):
                        for i, (h, w) in enumerate(((h_hi, d_hi[buf]), (h_hi, d_lo[buf]), (h_lo, d_hi[buf]))):
                            last = nc.tensor.matmul(ps[:, 5 + a, :], h[0:fn, f, a * P:(a + 1) * P], w[0:fn, f, :],
                                                    start=(f == 0 and i == 0), stop=(f == NF - 1 and i == 2),
                                                    skip_group_check=True)
                        if f == NF - 1:
                            last.then_inc(path.y_mm, 1)

            pe.wait_ge(consts_b, 6)
            turn(shared, 0)
            pe.wait_ge(both_done, 1)
            flat = both[:].rearrange("p t e -> p (t e)")
            nc.tensor.matmul(ps[:, 7, 0:P], tri[:], flat, start=True, stop=True)
            nc.tensor.matmul(ps[:, 7, P:2 * P], ones[:], flat, start=True, stop=True).then_inc(count_mm, 1)
            pe.wait_ge(e_loaded[0], NX)
            with pe.Fori(0, BLOCKS) as j:
                expert(shared, j, 0)
            pe.wait_ge(shared.xT_done, (BLOCKS + 1) * BA)
            turn(routed, 0)
            pe.wait_ge(shared.y_out, (BLOCKS + 1) * BA)
            pe.wait_ge(slots_ready, 1)
            with pe.Fori(0, EXPERTS // 2) as pair:
                for k in range(2):
                    pe.wait_ge(e_loaded[1 - k], pair * NX + NX * (k + 1))
                    pass_wait(pe)
                    lo, hi = block_range(pe, pair * 2 + k)
                    with pe.Fori(lo, hi) as j:
                        expert(routed, j, 1 - k)
            total = pe.value_load(first_i[0:1, EXPERTS:EXPERTS + 1], min_val=1, max_val=ROUTED_BLOCKS)
            pe.wait_ge(routed.xT_done, total * BA + BA)
            pe.wait_ge(routed.y_out, total * BA + BA)
            pass_wait(pe)
            pe.wait_ge(e_loaded[1], NX * (SLOTS // 2))
            with pe.Fori(BLOCKS, 2 * BLOCKS) as j:
                expert(shared, j, 1)

        @block.vector
        def _(dve):
            nc.vector.memset(qz[:], 0.0).then_inc(rope_link, 1)
            dve.wait_ge(rope_link, 1)
            dve.nop().then_inc(xn3_stored, 1)
            dve.wait_ge(x_loaded, 16)
            dve.wait_ge(consts, 3)
            dve.wait_ge(w_loaded, 16 * W_LOADS)

            def normalise(b, ln, stored):
                pass_wait(dve)
                for t in range(TT):
                    nc.vector.bn_stats(stats[:, t, :], acc[:, bass.ds(b * TT + t, 1), :]
                                       .rearrange("p o d -> p (o d)")).then_inc(ln_stats, 1)
                per = 2 * TT
                dve.wait_ge(ln_stats, ln * per + TT)
                pass_wait(dve)
                for t in range(TT):
                    nc.vector.bn_aggr(mv[:, t, :], stats[:, t, :]).then_inc(ln_stats, 1)
                dve.wait_ge(ln_stats, ln * per + per)
                nc.vector.tensor_scalar(veps[:], mv[:, :, 1], EPS, None, ALU.add).then_inc(ln_var, 1)
                if not isinstance(ln, int) or ln:
                    dve.wait_ge(ln_tr, ln * TT)
                if stored is not None:
                    dve.wait_ge(xn3_stored, stored)
                dve.wait_ge(ln_rstd, ln + 1)
                for t in range(TT):
                    nc.vector.tensor_scalar(xn[:, t, :], acc[:, bass.ds(b * TT + t, 1), :]
                                            .rearrange("p o d -> p (o d)"), mv[:, t, 0:1], rstd[:, t:t + 1],
                                            ALU.subtract, ALU.mult).then_inc(ln_xn, 1)

            swap = [i ^ 1 for i in range(32)]
            ROPE_LINKS = 3

            def rope(b, g):
                for i in range(2):
                    e = 2 * g + i
                    links = 1 + b * (2 * GROUPS * ROPE_LINKS) + e * ROPE_LINKS
                    raw = ps[:, QK_BANK, :]
                    dve.wait_ge(qk_mm, b * 2 * GROUPS + e + 1)
                    pass_wait(dve)
                    nc.vector.stream_shuffle(rope_sw[:], raw, swap).then_inc(rope_link, 1)
                    nc.vector.tensor_tensor(rope_c[:], raw, cos_sb[:], ALU.mult).then_inc(rope_link, 1)
                    dve.wait_ge(rope_link, links + 2)
                    dve.nop().then_inc(qk_used, 1)
                    nc.vector.tensor_tensor(rope_sw[:], rope_sw[:], sin_sb[:], ALU.mult).then_inc(rope_link, 1)
                    dve.wait_ge(rope_link, links + 3)
                    if i == 1:
                        nc.vector.tensor_tensor(kr[:, g % 2, :], rope_c[:], rope_sw[:], ALU.add).then_inc(rope_done, 1)
                    else:
                        for h in range(GH):
                            rows = slice(h * HDIM, (h + 1) * HDIM)
                            last = nc.vector.tensor_tensor(qz[rows, g % 2, h, :], rope_c[rows, :], rope_sw[rows, :],
                                                           ALU.add)
                        last.then_inc(rope_done, 1)
                    dve.wait_ge(rope_done, b * 2 * GROUPS + e + 1)

            def mask_and_max(b, n, h):
                i = n % TT
                w = (i + 1) * P
                dve.wait_ge(s_mm, b * HEADS * TT + GH * n + h + 1)
                if n >= WEIGH_LAG:
                    dve.wait_ge(pT_mm, b * HEADS * TT + GH * (n - WEIGH_LAG) + h + 1)
                pass_wait(dve)
                nc.vector.tensor_tensor_reduce(probs[n % TT][:, h, 0:w], ps[:, S_BANK + h % 2, 0:w],
                                               mask[:, TOKENS - w:], 1.0, LOWEST, ALU.add, ALU.max,
                                               mx[:, n % 2, h:h + 1]).then_inc(s_masked, 1)
                if h == GH - 1:
                    dve.wait_ge(s_masked, b * HEADS * TT + GH * n + GH)
                    nc.vector.tensor_scalar(nb[:, n % 2, :], mx[:, n % 2, :], -SCALE, None, ALU.mult).then_inc(nb_done, 1)

            def divide(b, n, h):
                w = (n % TT + 1) * P
                if h == 0:
                    dve.wait_ge(exp_done, b * HEADS * TT + GH * n + GH)
                    nc.vector.reciprocal(rsum[:, n % 2, :], sums[:, n % 2, :]).then_inc(rsum_done, 1)
                    dve.wait_ge(rsum_done, b * STEPS + n + 1)
                pr = probs[n % TT][:, h, 0:w]
                nc.vector.tensor_scalar(pr, pr, rsum[:, n % 2, h:h + 1], None, ALU.mult).then_inc(p_ready, 1)

            def add_to_residual(b, tiles, ready, added):
                for t in tiles:
                    dve.wait_ge(ready, b * TT + t + 1)
                    tile = acc[:, bass.ds(b * TT + t, 1), :].rearrange("p o d -> p (o d)")
                    nc.vector.tensor_tensor(tile, tile, ps[:, X_BANK + t % 2, :], ALU.add).then_inc(added, 1)
                if TT - 1 in tiles:
                    dve.wait_ge(added, b * TT + TT)

            def route(b):
                count = [0]

                def link(ins):
                    count[0] += 1
                    ins.then_inc(r_link, 1)
                    dve.wait_ge(r_link, b * ROUTER_LINKS + count[0])

                def wide(m):
                    return m.unsqueeze(2).to_broadcast([P, TT, EXPERTS])

                logits = ps[:, X_BANK, 0:TT * EXPERTS].rearrange("p (t e) -> p t e", e=EXPERTS)
                dve.wait_ge(r_mm, b + 1)
                link(nc.vector.tensor_reduce(r_m[:], logits, AX_X, ALU.max))
                nc.vector.tensor_tensor(r_t[:], logits, wide(r_m[:]), ALU.subtract).then_inc(r_shift, 1)
                dve.wait_ge(r_exp, b + 1)
                link(nc.vector.tensor_reduce(r_m[:], r_sc[:], AX_X, ALU.add))
                link(nc.vector.reciprocal(r_m[:], r_m[:]))
                link(nc.vector.tensor_tensor(r_sc[:], r_sc[:], wide(r_m[:]), ALU.mult))

                def pick(k, values, scratch):
                    tiles = bass.ds(b * TT, TT)
                    link(nc.vector.tensor_reduce(r_m[:], values, AX_X, ALU.max))
                    link(nc.vector.tensor_copy(weight[:, k, tiles], r_m[:]))
                    link(nc.vector.tensor_tensor(scratch, values, wide(r_m[:]), ALU.is_lt))
                    link(nc.vector.scalar_tensor_tensor(out=scratch, in0=scratch, scalar=float(EXPERTS),
                                                        in1=iota8[:], op0=ALU.mult, op1=ALU.add))
                    link(nc.vector.tensor_reduce(r_m[:], scratch, AX_X, ALU.min))
                    link(nc.vector.tensor_tensor(r_oh[:], iota8[:], wide(r_m[:]), ALU.is_equal))
                    link(nc.vector.tensor_copy(onehot[:, k, tiles, :], r_oh[:]))

                pick(0, r_sc[:], r_t[:])
                link(nc.vector.scalar_tensor_tensor(out=r_t[:], in0=r_oh[:], scalar=-2.0, in1=r_sc[:],
                                                    op0=ALU.mult, op1=ALU.add))
                pick(1, r_t[:], r_t[:])
                assert count[0] == ROUTER_LINKS, count

            def cross(p, ln, r):
                if r in ENERGIES:
                    for t in ENERGIES[r]:
                        dve.wait_ge(e_mm, p * TT + t + 1)
                        nc.vector.tensor_reduce(a_mx[:, t:t + 1], ps[:, X_BANK + t % 2, :], AX_X, ALU.max)\
                            .then_inc(e_max, 1)
                        dve.wait_ge(e_max, p * TT + t + 1)
                        nc.vector.tensor_scalar(a_nb[:, t:t + 1], a_mx[:, t:t + 1], -1.0, None, ALU.mult)\
                            .then_inc(e_nb, 1)
                if r in TURNS:
                    for t in TURNS[r]:
                        dve.wait_ge(e_exp, p * TT + t + 1)
                        nc.vector.reciprocal(a_rsum[:, t:t + 1], a_sums[:, t:t + 1]).then_inc(e_rsum, 1)
                        dve.wait_ge(e_rsum, p * TT + t + 1)
                        nc.vector.tensor_scalar(att[:, t % 2, :], att[:, t % 2, :], a_rsum[:, t:t + 1], None,
                                                ALU.mult).then_inc(a_ready, 1)
                if r in MIXES:
                    add_to_residual(p, MIXES[r], xm_mm, xm_added)
                    if TT - 1 in MIXES[r]:
                        normalise(p, ln + 1, None)
                if r == ROUTE:
                    route(p)

            def attend(b, ln, p):
                normalise(b, ln, None if p is None else p * 16 + 1)
                if p is not None:
                    add_to_residual(p, range(TT), proj_mm, proj_added)
                rope(b, 0)
                if p is not None:
                    normalise(p, ln + 1, None)
                for r in range(STEPS + WEIGH_LAG):
                    for h in range(GH):
                        if 0 <= r - DIVIDE_LAG < STEPS:
                            divide(b, r - DIVIDE_LAG, h)
                        if r < STEPS:
                            mask_and_max(b, r, h)
                    if r % TT == 2 and r // TT + 1 < GROUPS:
                        rope(b, r // TT + 1)
                    if p is not None:
                        cross(p, ln + 1, r)

            dve.nop().then_inc(r_shift, 1)
            attend(0, 0, None)
            with dve.Fori(1, BATCHES) as b:
                attend(b, b * 3 - 2, b - 1)
            add_to_residual(BATCHES - 1, range(TT), proj_mm, proj_added)
            normalise(BATCHES - 1, 3 * BATCHES - 2, 16 * (BATCHES - 1) + 1)
            for r in range(ROUTE + 1):
                cross(BATCHES - 1, 3 * BATCHES - 2, r)

            for k in range(2):
                dve.nop().then_inc(e_used[k], 1)
                dve.nop().then_inc(picked_used[k], 1)
            for path in (shared, routed):
                dve.nop().then_inc(path.h_done, NF)
                dve.nop().then_inc(path.y_out, BA)
            dve.nop().then_inc(y_stored, 16)

            def dispatch():
                count = [0]

                def link(ins):
                    count[0] += 1
                    ins.then_inc(d_link, 1)
                    dve.wait_ge(d_link, count[0])

                dve.wait_ge(xn3_stored, 16 * BATCHES + 1)
                nc.vector.tensor_tensor(both[:], onehot[:, 0], onehot[:, 1], ALU.add).then_inc(both_done, 1)
                link(nc.vector.memset(before[:, 0, :], 0.0))
                link(nc.vector.memset(first[:, 0:1], 0.0))
                dve.wait_ge(count_mm, 1)
                dve.wait_ge(consts_b, 6)
                within = ps[:, 7, 0:P].rearrange("p (t e) -> p t e", e=EXPERTS)
                link(nc.vector.tensor_copy(tots[:], ps[:, 7, P:2 * P].rearrange("p (t e) -> p t e", e=EXPERTS)))
                for t in range(TILES):
                    link(nc.vector.tensor_tensor(before[:, t + 1, :], before[:, t, :], tots[:, t, :], ALU.add))
                link(nc.vector.tensor_tensor(more[:], before[:, TILES, :].unsqueeze(2)
                                             .to_broadcast([P, EXPERTS, BLOCKS - 1]), steps[:], ALU.is_gt))
                link(nc.vector.tensor_reduce(nblk[:], more[:], AX_X, ALU.add))
                link(nc.vector.tensor_scalar(nblk[:], nblk[:], 1.0, None, ALU.add))
                for e in range(EXPERTS):
                    link(nc.vector.tensor_tensor(first[:, e + 1:e + 2], first[:, e:e + 1], nblk[:, e:e + 1], ALU.add))
                link(nc.vector.tensor_copy(first_i[:], first[:]))
                link(nc.vector.tensor_scalar(first_row[:], first[:, 0:EXPERTS], float(BT), None, ALU.mult))
                link(nc.vector.tensor_tensor(row[:], within, before[:, 0:TILES, :], ALU.add))
                link(nc.vector.tensor_tensor(row[:], row[:], first_row[:].unsqueeze(1)
                                             .to_broadcast([P, TILES, EXPERTS]), ALU.add))
                for k in range(2):
                    link(nc.vector.tensor_tensor(both[:], onehot[:, k], row[:], ALU.mult))
                    link(nc.vector.tensor_reduce(row_k[:, k, :], both[:], AX_X, ALU.add))
                link(nc.vector.tensor_copy(slot_i[:], row_k[:]))
                link(nc.vector.tensor_scalar(place_lo[:], slot_i[:], P - 1, None, ALU.bitwise_and))
                link(nc.vector.tensor_scalar(place_hi[:], slot_i[:], P.bit_length() - 1, None,
                                             ALU.arith_shift_right))
                nc.vector.scalar_tensor_tensor(out=place_i[:], in0=place_lo[:], scalar=float(SLOT_COLS),
                                               in1=place_hi[:], op0=ALU.mult, op1=ALU.add).then_inc(slots_ready, 1)

            def turn(path, block):
                for a in range(BA):
                    dve.wait_ge(path.xT_hi_done, block * BA + a + 1)
                    cols = slice(a * P, (a + 1) * P)
                    nc.vector.tensor_tensor(path.xT_lo[:, :, cols], ps[:, 3 + a, :].rearrange("p (c n) -> p c n", c=CC),
                                            path.xT_hi[:, :, cols].bitcast(F32), ALU.subtract).then_inc(path.xT_done, 1)

            def expert(path, j, put):
                for f in range(NF + 1):
                    if f < NF:
                        fn = HCHUNKS[f][1]
                        dve.wait_ge(path.sg_done, j * NF + f + 1)
                        nc.vector.tensor_tensor(hf[0:fn, f, :], sg[0:fn, f, :], ps[0:fn, f, BT:2 * BT], ALU.mult)\
                            .then_inc(path.h_done, 1)
                    if f >= 1:
                        fn = HCHUNKS[f - 1][1]
                        dve.wait_ge(path.h_hi_done, j * NF + f)
                        nc.vector.tensor_tensor(h_lo[0:fn, f - 1, :], hf[0:fn, f - 1, :],
                                                h_hi[0:fn, f - 1, :].bitcast(F32), ALU.subtract)\
                            .then_inc(path.hT_done, 1)
                turn(path, j + 1)
                for a in range(BA):
                    dve.wait_ge(path.y_mm, j * BA + a + 1)
                    put(a)

            def tile_of(j, a):
                return acc[:, bass.ds(j * BA + a, 1), :].rearrange("p o d -> p (o d)")

            turn(shared, 0)
            dispatch()
            with dve.Fori(0, BLOCKS) as j:
                def add(a):
                    tile = tile_of(j, a)
                    nc.vector.tensor_tensor(tile, tile, ps[:, 5 + a, :], ALU.add).then_inc(shared.y_out, 1)

                expert(shared, j, add)
            dve.nop().then_inc(e_used[0], 1)
            turn(routed, 0)
            with dve.Fori(0, EXPERTS // 2) as pair:
                for k in range(2):
                    lo, hi = block_range(dve, pair * 2 + k)
                    with dve.Fori(lo, hi) as j:
                        def store(a):
                            if a == 0:
                                dve.wait_ge(y_stored, j * 16 + 16)
                            nc.vector.tensor_copy(y_sb[:, a, :], ps[:, 5 + a, :]).then_inc(routed.y_out, 1)

                        expert(routed, j, store)
                    dve.nop().then_inc(e_used[1 - k], 1)
            dve.wait_ge(shared.y_out, (BLOCKS + 1) * BA)
            with dve.Fori(0, BLOCKS) as j:
                def add(a):
                    tile = tile_of(j, a)
                    nc.vector.tensor_tensor(tile, tile, ps[:, 5 + a, :], ALU.add).then_inc(shared.y_out, 1)

                expert(shared, j + BLOCKS, add)
                dve.wait_ge(shared.y_out, j * BA + (BLOCKS + 2) * BA)
                for k in range(2):
                    for a in range(BA):
                        if k == 0:
                            dve.wait_ge(pick_loaded[a], j * 32 + 32)
                        tile = tile_of(j, a)
                        nc.vector.scalar_tensor_tensor(
                            out=tile, in0=picked[:, a, k, :], scalar=weight[:, k, bass.ds(j * BA + a, 1)], in1=tile,
                            op0=ALU.mult, op1=ALU.add).then_inc(acc_link, 1)
                    dve.wait_ge(acc_link, j * (2 * BA) + (k + 1) * BA)
                dve.nop().then_inc(tile_done, 1)
                for a in range(BA):
                    dve.nop().then_inc(picked_used[a], 1)


def rope_tables():
    theta = (1.0 / np.float32(10000.0) ** (np.arange(0, HDIM, 2, dtype=np.float32) / np.float32(HDIM))).astype(np.float32)
    angle = np.outer(np.arange(TOKENS, dtype=np.float32), theta).astype(np.float32)
    by_feature = np.repeat(np.arange(HDIM // 2), 2)
    sign = np.tile(np.array([-1.0, 1.0], np.float32), HDIM // 2)
    cos = np.cos(angle)[:, by_feature].T
    sin = (np.sin(angle)[:, by_feature] * sign).T
    return (np.ascontiguousarray(np.tile(cos, (GH, 1)), np.float32),
            np.ascontiguousarray(np.tile(sin, (GH, 1)), np.float32))


def kernel(**inputs):
    import concourse.bacc as _bacc
    from concourse.bass_utils import run_bass_kernel_spmd as _run

    i = {k: np.asarray(v) for k, v in inputs.items()}
    cos, sin = rope_tables()

    routed_gu = np.stack([i["L0_ffn_We_gate"], i["L0_ffn_We_up"]], axis=1)
    gate, up = (np.split(i[n], SHARED, axis=1) for n in ("L0_ffn_Ws_gate", "L0_ffn_Ws_up"))
    first_gu, second_gu = (np.stack([g, u])[None] for g, u in zip(gate, up))
    first_d, second_d = (d[None] for d in np.split(i["L0_ffn_Ws_down"], SHARED, axis=0))
    arrays = {
        "x": i["x"].reshape(BATCHES * TOKENS, DIM),
        "ctxT": i["ctx_1024"].transpose(0, 2, 1),
        "waT": i["L0_attn_w_atten"].T, "wpT": i["L0_attn_w_proj"].T,
        "wqT": i["L0_xattn_Wq"].T, "wkT": i["L0_xattn_Wk"].T,
        "bq": i["L0_xattn_bq"].reshape(P, 1), "bk": i["L0_xattn_bk"].reshape(P, 1),
        "wr": i["L0_ffn_W_router"],
        "we": np.concatenate([w.reshape(-1) for w in (first_gu, routed_gu, second_gu, first_d,
                                                      i["L0_ffn_We_down"], second_d)]),
        "cosT": cos, "sinT": sin,
    }
    arrays = {f"in_{k}": np.ascontiguousarray(v) for k, v in arrays.items()}
    nc = _bacc.Bacc("TRN2", target_bir_lowering=False, num_devices=1)
    args = [nc.dram_tensor(k, v.shape, mybir.dt.from_np(v.dtype), kind="ExternalInput").ap() for k, v in arrays.items()]
    out = nc.dram_tensor("out", (BATCHES * TOKENS, DIM), F32, kind="ExternalOutput").ap()
    build(nc, *args, out)
    r = _run(nc, [arrays], core_ids=[0])
    return r.results[0]["out"].reshape(BATCHES, TOKENS, DIM)
```

```python
from contextlib import ExitStack

import numpy as np

import concourse.bass as bass
from concourse import mybir

P = 128
F32 = mybir.dt.float32
F32R = mybir.dt.float32r
I32 = mybir.dt.int32
ALU = mybir.AluOpType
ACT = mybir.ActivationFunctionType
AX_X = mybir.AxisListType.X

BATCHES, TOKENS, DIM = 4, 512, 512
CTX = 256
HEADS, HDIM = 16, 32
EXPERTS, EDIM = 8, 352
SHARED = 2
SLOTS = EXPERTS + SHARED
TT = TOKENS // P
TILES = BATCHES * TT
CC = DIM // P
GROUPS = HEADS * HDIM // P
GH = P // HDIM
STEPS = GROUPS * TT
BT = 256
BA = BT // P
BLOCKS = BATCHES * TOKENS // BT
ROUTED_BLOCKS = 2 * BLOCKS + EXPERTS - 1
SLOT_COLS = (ROUTED_BLOCKS + 1) * BA
GU_SIZE, D_SIZE = SLOTS * 2 * DIM * EDIM, SLOTS * EDIM * DIM
EXP_LAG, DIVIDE_LAG, TURN_LAG, WEIGH_LAG = 1, 2, 3, 4
HCHUNKS = [(f * P, min(P, EDIM - f * P)) for f in range((EDIM + P - 1) // P)]
NF = len(HCHUNKS)
EPS = 1e-5
SCALE = float(HDIM) ** -0.5
MASKED = -1e30
LOWEST = -3e38


def build(nc, x, ctxT, waT, wpT, wqT, wkT, bq, bk, wr, we, cosT, sinT, out):
    with ExitStack() as stack:
        def sb(name, shape, dt=F32):
            return stack.enter_context(nc.sbuf_tensor(name, shape, dt))

        def sem(name):
            return stack.enter_context(nc.semaphore(name))

        acc = sb("acc", [P, TILES, DIM])
        ident = sb("ident", [P, P])
        onehot = sb("onehot", [P, 2, TILES, EXPERTS])
        weight = sb("weight", [P, 2, TILES])
        slot_i = sb("slot_i", [P, 2, TILES], I32)
        first_i = sb("first_i", [P, EXPERTS + 1], I32)
        xn3_d = nc.dram_tensor("xn3_d", [BATCHES * TOKENS, DIM], F32).ap()
        token_d = nc.dram_tensor("token_d", [SLOT_COLS * P, 1], I32).ap()
        y_d = nc.dram_tensor("y_d", [(ROUTED_BLOCKS + 1) * BT, DIM], F32).ap()

        attention = stack.enter_context(ExitStack())

        def sb(name, shape, dt=F32):
            return attention.enter_context(nc.sbuf_tensor(name, shape, dt))

        wa_sb = sb("wa_sb", [P, CC, 3 * DIM])
        cos_sb = sb("cos_sb", [P, TOKENS])
        sin_sb = sb("sin_sb", [P, TOKENS])
        xnT = sb("xnT", [P, CC, TOKENS])
        rope_a = [sb(f"rope_a{i}", [P, TOKENS]) for i in range(2)]
        rope_b = [sb(f"rope_b{i}", [P, TOKENS]) for i in range(2)]
        xn1 = sb("xn1", [P, TT, DIM])
        assert (CC * 3 + 2 + CC + 4 + TT) * TOKENS >= 3 * (2 * CC * EDIM + NF * DIM)
        mask = sb("mask", [P, TOKENS])
        v_sb = sb("v_sb", [P, TT, DIM])
        qs = sb("qs", [3 * HDIM, 2, GH, TOKENS], F32R)
        ks = sb("ks", [3 * HDIM, 2, GH, TOKENS], F32R)
        assert WEIGH_LAG == TT
        probs = [sb(f"probs{i}", [P, GH, (i + 1) * P]) for i in range(TT)]
        probsT = [sb(f"probsT{i}", [P, GH, (TT - 1 + i) * P]) for i in range(2)]
        mx = sb("mx", [P, 2, GH])
        nb = sb("nb", [P, 2, GH])
        sums = sb("sums", [P, 2, GH])
        rsum = sb("rsum", [P, 2, GH])
        ctx_sb = sb("ctx_sb", [P, CTX // P, TOKENS])
        wp_sb = sb("wp_sb", [P, CC, DIM])
        wq_sb = sb("wq_sb", [P, CTX // P, P])
        wk_sb = sb("wk_sb", [P, CTX // P, P])
        wr_sb = sb("wr_sb", [P, CC, EXPERTS])
        bias_sb = sb("bias_sb", [P, 2])
        iota8 = sb("iota8", [P, TT, EXPERTS])
        stats = sb("stats", [P, TT, 6])
        mv = sb("mv", [P, TT, 2])
        veps = sb("veps", [P, TT])
        rstd = sb("rstd", [P, TT])
        power = sb("power", [P, TT])
        xn = sb("xn", [P, TT, DIM])
        yT = sb("yT", [P, GROUPS, TOKENS])
        q2 = sb("q2", [P, TOKENS])
        k2 = sb("k2", [P, TOKENS])
        xn_xT = sb("xn_xT", [P, CC, TOKENS])
        att = ctx_sb
        attT = xn
        a_mx = sb("a_mx", [P, TT])
        a_nb = sb("a_nb", [P, TT])
        a_sums = sb("a_sums", [P, TT])
        a_rsum = sb("a_rsum", [P, TT])
        r_sc = sb("r_sc", [P, TT, EXPERTS])
        r_t = sb("r_t", [P, TT, EXPERTS])
        r_m = sb("r_m", [P, TT])
        r_oh = sb("r_oh", [P, TT, EXPERTS])
        attention.close()

        def sb(name, shape, dt=F32):
            return stack.enter_context(nc.sbuf_tensor(name, shape, dt))

        gu_raw = sb("gu_raw", [P, 2 * CC, EDIM])
        d_raw = sb("d_raw", [P, NF, DIM])
        gu_hi, d_hi, gu_lo, d_lo = [], [], [], []
        for k in range(2):
            gu_hi.append(sb(f"gu_hi{k}", [P, 2 * CC, EDIM], F32R))
            d_hi.append(sb(f"d_hi{k}", [P, NF, DIM], F32R))
            gu_lo.append(sb(f"gu_lo{k}", [P, 2 * CC, EDIM], F32R))
            d_lo.append(sb(f"d_lo{k}", [P, NF, DIM], F32R))
        sg = sb("sg", [P, NF, BT])
        hf = sb("hf", [P, NF, BT])
        h_hi = sb("h_hi", [P, NF, BT], F32R)
        h_lo = sb("h_lo", [P, NF, BT], F32R)
        y_sb = sb("y_sb", [P, BA, DIM])
        class Path:
            def __init__(self, name):
                self.x = sb(name + "_x", [P, BA, DIM])
                self.xT_hi = sb(name + "_xT_hi", [P, CC, BT], F32R)
                self.xT_lo = sb(name + "_xT_lo", [P, CC, BT], F32R)
                self.x_loaded = sem(name + "_x_loaded")
                self.x_turned = sem(name + "_x_turned")
                self.xT_hi_done = sem(name + "_xT_hi_done")
                self.xT_done = sem(name + "_xT_done")
                self.gu_mm = sem(name + "_gu_mm")
                self.sg_done = sem(name + "_sg_done")
                self.h_done = sem(name + "_h_done")
                self.h_hi_done = sem(name + "_h_hi_done")
                self.hT_done = sem(name + "_hT_done")
                self.y_mm = sem(name + "_y_mm")
                self.y_out = sem(name + "_y_out")

        shared = Path("shared")
        picked = sb("picked", [P, 2, 2, DIM])
        pick_i = sb("pick_i", [P, 2, 2], I32)
        tri = sb("tri", [P, P])
        ones = sb("ones", [P, P])
        zero_row = sb("zero_row", [P, DIM])
        tok_i = sb("tok_i", [P, TILES], I32)
        table_zero = sb("table_zero", [P, SLOT_COLS], I32)
        table = sb("table", [P, SLOT_COLS], I32)
        table_cur = sb("table_cur", [P, BA], I32)
        both = sb("both", [P, TILES, EXPERTS])
        tots = sb("tots", [P, TILES, EXPERTS])
        before = sb("before", [P, TILES + 1, EXPERTS])
        steps = sb("steps", [P, EXPERTS, BLOCKS - 1])
        more = sb("more", [P, EXPERTS, BLOCKS - 1])
        nblk = sb("nblk", [P, EXPERTS])
        first = sb("first", [P, EXPERTS + 1])
        first_row = sb("first_row", [P, EXPERTS])
        row = sb("row", [P, TILES, EXPERTS])
        row_k = sb("row_k", [P, 2, TILES])
        place_lo = sb("place_lo", [P, 2, TILES], I32)
        place_hi = sb("place_hi", [P, 2, TILES], I32)
        place_i = sb("place_i", [P, 2, TILES], I32)
        routed = Path("routed")
        shared.loads, routed.loads = 1, BA

        ps = stack.enter_context(nc.psum_tensor("ps", [P, 8, 512], F32))
        S_BANK, T_BANK, O_BANK, QK_BANK, X_BANK = 0, 2, 4, 5, 6
        PROJ_BANKS = (S_BANK, S_BANK + 1, X_BANK, X_BANK + 1)
        NEXT_BANK = QK_BANK
        V_BANKS = (O_BANK, T_BANK, T_BANK + 1, O_BANK)
        XT_BANK, Y_BANK, COUNT_BANK = 3, 5, 7
        VALUES = {3 * t + at: (t, chunks) for t in range(TT) for at, chunks in enumerate(((0, 1), (2,), (3,)))}
        VALUE_COPIES = {3 * t + 3: t for t in range(TT)}
        QK_PLACES = {0: (0, (0, 1)), 1: (0, (2, 3)), 3: (1, (0, 1)), 4: (1, (2, 3))}
        ROPE_PLACES = {2: (0, (0,)), 4: (0, (1,)), 5: (1, (0,)), 7: (1, (1,))}
        CTX_QK = {1: 0, 2: 1}
        LN2_TURNS = {4: (0,), 5: (1,), 7: (2,), 8: (3,)}
        ENERGIES = {10: (0,), 11: (1,), 20: (2,), 21: (3,)}
        E_MAX, E_EXP, E_DIVIDE, E_TURN, E_COPY = 1, 2, 4, 5, 7
        MIXES = {28 + TT * t + c: (t, c) for t in range(TT) for c in range(TT)}
        MIX_ADDS = {28 + TT * t + TT: (t,) for t in range(TT)}
        LN2_SCALES = {0: 0, 1: 1, 2: 2, 3: 3}
        LN3_STATS = {33: 0, 37: 1, 41: 2, 45: 3}
        LN3_VARIANCE = 46
        LN3_SCALES = {48: 0, 49: 1, 50: 2, 51: 3}
        LN3_TURNS = {50: (0,), 51: (1,), 53: (2,), 54: (3,)}
        ROUTES = {56 + t: t for t in range(TT)}
        ROUTE, END_ROUTE = 64, 60
        CROSS_PLACES = END_ROUTE + 2
        NEXT_STATS = {22: (0, 1), 23: (2, 3)}
        NEXT_VARIANCE = 24
        NEXT_SCALES = {26: 0, 27: 1, 29: 2, 30: 3}
        NEXT_TURNS = {40: 0, 42: 1, 44: 2, 46: 3}
        NEXT_QK = 48
        PROJECTIONS = {64 + (GROUPS - 1) * t + g: (t, g) for t in range(TT) for g in range(GROUPS - 1)}
        SPLIT_PLACES = (56, 60, 64, 68, 72, 76)
        EARLY_BLOCKS, EARLY_PERIOD = 5, 7
        EARLY_GU = {1: 0, 2: 1, 3: 2}
        EARLY_TURN = 4
        EARLY_Y = {7: 0, 8: 1}
        EARLY_PLACES = (EARLY_BLOCKS - 1) * EARLY_PERIOD + 10
        COUNT_PLACE = CROSS_PLACES // 2

        def early(place, steps):
            for j in range(EARLY_BLOCKS):
                if place - j * EARLY_PERIOD in steps:
                    yield j, steps[place - j * EARLY_PERIOD]

        def later(steps, by):
            return {place + by: value for place, value in steps.items()}

        def second_ln(b):
            return b * 3 - 1

        def next_ln(b):
            return 1 if isinstance(b, int) and b == 0 else b * 3

        def third_ln(b, last):
            return b * 3 if last else b * 3 + 1

        def route_place(p):
            return END_ROUTE if isinstance(p, int) and p == BATCHES - 1 else ROUTE

        END_LN = 3 * BATCHES - 2

        def queries_keys(place, b, last, table):
            group, at = divmod(place, STEPS)
            if at in table and group + 1 < GROUPS:
                yield (b, group + 1) + table[at]
            if place - NEXT_QK in table and not last:
                yield (b + 1, 0) + table[place - NEXT_QK]

        x_loaded = sem("x_loaded")
        wa_loaded = sem("wa_loaded")
        tables_loaded = sem("tables_loaded")
        w_loaded = sem("w_loaded")
        ctx_loaded = sem("ctx_loaded")
        consts = sem("consts")
        zeroed = sem("zeroed")
        ln_stats = sem("ln_stats")
        ln_var = sem("ln_var")
        ln_rstd = sem("ln_rstd")
        ln_xn = sem("ln_xn")
        ln_tr = sem("ln_tr")
        ln_xnT = sem("ln_xnT")
        v_mm = sem("v_mm")
        v_done = sem("v_done")
        qk_mm = sem("qk_mm")
        qk_used = sem("qk_used")
        rope_link = sem("rope_link")
        rope_sine = sem("rope_sine")
        rope_done = sem("rope_done")
        stacked = sem("stacked")
        s_mm = sem("s_mm")
        s_masked = sem("s_masked")
        nb_done = sem("nb_done")
        exp_done = sem("exp_done")
        rsum_done = sem("rsum_done")
        p_ready = sem("p_ready")
        pT_mm = sem("pT_mm")
        pT_done = sem("pT_done")
        pv_mm = sem("pv_mm")
        yT_done = sem("yT_done")
        proj_mm = sem("proj_mm")
        proj_added = sem("proj_added")
        qk2_mm = sem("qk2_mm")
        qk2_done = sem("qk2_done")
        e_mm = sem("e_mm")
        e_max = sem("e_max")
        e_nb = sem("e_nb")
        e_exp = sem("e_exp")
        e_rsum = sem("e_rsum")
        a_ready = sem("a_ready")
        aT_mm = sem("aT_mm")
        aT_done = sem("aT_done")
        xm_mm = sem("xm_mm")
        xm_added = sem("xm_added")
        xn3_stored = sem("xn3_stored")
        r_mm = sem("r_mm")
        r_link = sem("r_link")
        r_shift = sem("r_shift")
        r_exp = sem("r_exp")
        raw_loaded = sem("raw_loaded")
        hi_made = sem("hi_made")
        lo_made = sem("lo_made")
        slot_done = sem("slot_done")
        consts_b = sem("consts_b")
        both_done = sem("both_done")
        count_mm = sem("count_mm")
        d_link = sem("d_link")
        slots_ready = sem("slots_ready")
        table_cleared = sem("table_cleared")
        table_written = sem("table_written")
        table_loaded = sem("table_loaded")
        cur_copied = sem("cur_copied")
        y_stored = sem("y_stored")
        pick_copied = sem("pick_copied")
        pick_loaded = [sem("pick_loaded0"), sem("pick_loaded1")]
        picked_used = [sem("picked_used0"), sem("picked_used1")]
        acc_link = sem("acc_link")
        tile_done = sem("tile_done")
        stored = sem("stored")

        waited = sem("waited")

        def pass_wait(eng):
            eng.nop().then_inc(waited, 1)

        W_LOADS = 7
        STACK = 2 * 3 * GH * 16
        ROUTER_LINKS = 19
        ROPE_LINKS = 4

        def weight_chunks(gu, d):
            return ([gu[:, i:i + 2, :] for i in range(0, 2 * CC, 2)] +
                    [d[:, 0:NF - 1, :], d[0:HCHUNKS[-1][1], NF - 1, :]])

        WC = CC + 2
        RAW = 3 * 16

        def block_range(eng, e):
            lo = eng.value_load(first_i[0:1, bass.ds(e, 1)], min_val=0, max_val=ROUTED_BLOCKS - 1)
            hi = eng.value_load(first_i[0:1, bass.ds(e + 1, 1)], min_val=1, max_val=ROUTED_BLOCKS)
            return lo, hi

        x_v = x.rearrange("(b t p) d -> b p t d", p=P, t=TT)
        out_v = out.rearrange("(t p) d -> p t d", p=P)
        xn3_v = xn3_d.rearrange("(t p) d -> p t d", p=P)

        ctx_v = ctxT.rearrange("b (c p) n -> p (b c) n", p=P)
        NCTX = CTX // P

        block = stack.enter_context(nc.Block())

        @block.sync
        def _(sp):
            sp.dma_start(acc[:, 0:TT, :], x_v[0]).then_inc(x_loaded, 16)
            def load_context(p):
                sp.wait_ge(xn3_stored, p * 16 + 1)
                sp.dma_start(ctx_sb[:], ctx_v[:, bass.ds(p * NCTX, NCTX), :]).then_inc(ctx_loaded, 16)

            def stack_heads(b, g):
                for i, (stacks, parts) in enumerate(((qs, (rope_b, rope_b, rope_a)), (ks, (rope_b, rope_a, rope_b)))):
                    sp.wait_ge(rope_done, b * (2 * GROUPS) + (2 * g + i + 1))
                    for j, part in enumerate(parts):
                        for h in range(GH):
                            sp.dma_start(stacks[j * HDIM:(j + 1) * HDIM, g % 2, h, :].bitcast(F32),
                                         part[i][h * HDIM:(h + 1) * HDIM, :]).then_inc(stacked, 16)

            def store_xn3(p, ln):
                sp.wait_ge(ln_xn, ln * TT + TT)
                sp.dma_start(xn3_v[:, bass.ds(p * TT, TT), :], xn[:]).then_inc(xn3_stored, 16)

            loads = [(wa_loaded, [(wa_sb[:], waT.rearrange("(c p) n -> p c n", p=P))]),
                     (tables_loaded, [(cos_sb[:], cosT), (sin_sb[:], sinT)]),
                     (w_loaded, [(wp_sb[:], wpT.rearrange("(c p) n -> p c n", p=P)),
                                 (wq_sb[:], wqT.rearrange("(c p) n -> p c n", p=P)),
                                 (wk_sb[:], wkT.rearrange("(c p) n -> p c n", p=P)),
                                 (wr_sb[:], wr.rearrange("(c p) n -> p c n", p=P)),
                                 (bias_sb[:, 0:1], bq), (bias_sb[:, 1:2], bk),
                                 (acc[:, TT:TILES, :], x[TT * P:, :].rearrange("(t p) d -> p t d", p=P))])]
            for loaded, moves in loads:
                if loaded is w_loaded:
                    stack_heads(0, 0)
                for dst, src in moves:
                    sp.dma_start(dst, src).then_inc(loaded, 16)

            gu_v = we[0:GU_SIZE].rearrange("(r p n) -> p r n", p=P, n=EDIM)
            d_v = we[GU_SIZE:GU_SIZE + D_SIZE].rearrange("(r n) -> r n", n=DIM)

            def load_weights(s):
                if not isinstance(s, int) or s:
                    sp.wait_ge(lo_made, s * WC)
                f0, fn = HCHUNKS[-1]
                sp.dma_start(gu_raw[:], gu_v[:, bass.ds(s * (2 * CC), 2 * CC), :]).then_inc(raw_loaded, 16)
                sp.dma_start(d_raw[:, 0:NF - 1, :], d_v[bass.ds(s * EDIM, (NF - 1) * P), :]
                             .rearrange("(f p) n -> p f n", p=P)).then_inc(raw_loaded, 16)
                sp.dma_start(d_raw[0:fn, NF - 1, :], d_v[bass.ds(s * EDIM + f0, fn), :]).then_inc(raw_loaded, 16)

            def beside(b, p, last=False):
                if p is not None:
                    load_context(p)
                for g in range(1, GROUPS):
                    stack_heads(b, g)
                if last:
                    load_weights(0)
                if p is not None:
                    store_xn3(p, third_ln(b, last))
                if not last:
                    stack_heads(b + 1, 0)

            beside(0, None)
            with sp.Fori(1, BATCHES - 1) as b:
                beside(b, b - 1)
            beside(BATCHES - 1, BATCHES - 2, last=True)
            def load_tokens(block):
                sp.dma_start(shared.x[:], xn3_v[:, bass.ds(block * BA, BA), :]).then_inc(shared.x_loaded, 16)

            load_context(BATCHES - 1)
            sp.wait_ge(yT_done, BATCHES * GROUPS)
            load_tokens(0)
            load_weights(1)
            for j in range(EARLY_BLOCKS):
                sp.wait_ge(shared.x_turned, j * BA + BA)
                load_tokens(j + 1)
            store_xn3(BATCHES - 1, END_LN + 1)
            sp.wait_ge(consts_b, 6)
            sp.dma_start(token_d.rearrange("(p n) o -> p (n o)", p=P), table_zero[:]).then_inc(table_cleared, 16)
            sp.wait_ge(xn3_stored, 16 * BATCHES + 1)
            for j in range(EARLY_BLOCKS, BLOCKS):
                sp.wait_ge(shared.x_turned, j * BA + BA)
                load_tokens((j + 1) % BLOCKS)
            load_weights(2)
            sp.wait_ge(slots_ready, 1)

            def store_blocks(e):
                lo, hi = block_range(sp, e)
                with sp.Fori(lo, hi) as j:
                    sp.wait_ge(routed.y_out, j * BA + (BA + 2))
                    sp.dma_start(y_d[bass.ds(j * BT, BT), :].rearrange("(a p) d -> p a d", p=P), y_sb[:])\
                        .then_inc(y_stored, 16)

            with sp.Fori(0, EXPERTS - 1) as e:
                load_weights(e + 3)
                store_blocks(e)
            store_blocks(EXPERTS - 1)
            total = sp.value_load(first_i[0:1, EXPERTS:EXPERTS + 1], min_val=1, max_val=ROUTED_BLOCKS)
            with sp.Fori(total, ROUTED_BLOCKS + 1) as j:
                sp.dma_start(y_d[bass.ds(j * BT, BT), :].rearrange("(a p) d -> p a d", p=P),
                             zero_row[:].unsqueeze(1).to_broadcast([P, BA, DIM])).then_inc(y_stored, 16)
            def store_out(j):
                sp.wait_ge(tile_done, j + 1)
                sp.dma_start(out_v[:, bass.ds(j * BA, BA), :], acc[:, bass.ds(j * BA, BA), :]).then_inc(stored, 16)

            sp.wait_ge(shared.x_turned, (BLOCKS + 1) * BA)
            load_tokens(1)
            with sp.Fori(0, BLOCKS - 1) as j:
                sp.wait_ge(shared.x_turned, j * BA + (BLOCKS + 2) * BA)
                load_tokens((j + 2) % BLOCKS)
                store_out(j)
            store_out(BLOCKS - 1)
            sp.wait_ge(stored, 16 * BLOCKS)

        @block.gpsimd
        def _(pool):
            nc.gpsimd.memset(ident[:], 0.0).then_inc(zeroed, 1)
            nc.gpsimd.memset(mask[:], 0.0).then_inc(zeroed, 1)
            nc.gpsimd.memset(power[:], -0.5).then_inc(zeroed, 1)
            pool.wait_ge(zeroed, 3)
            nc.gpsimd.affine_select(out=ident[:], in_=ident[:], compare_op=ALU.not_equal, fill=1.0, base=0,
                                    pattern=[[-1, P]], channel_multiplier=1).then_inc(consts, 1)
            diag = mask[:, TOKENS - P:TOKENS]
            nc.gpsimd.affine_select(out=diag, in_=diag, compare_op=ALU.is_ge, fill=MASKED, base=0,
                                    pattern=[[-1, P]], channel_multiplier=1).then_inc(consts, 1)
            nc.gpsimd.iota(iota8[:], pattern=[[0, TT], [1, EXPERTS]], base=0, channel_multiplier=0,
                           allow_small_or_imprecise_dtypes=True).then_inc(consts, 1)

            def root(ln):
                pool.wait_ge(ln_var, ln + 1)
                nc.gpsimd.tensor_tensor(rstd[:], veps[:], power[:], ALU.pow).then_inc(ln_rstd, 1)

            def rotate(b, g):
                for i in range(2):
                    e = b * (2 * GROUPS) + (2 * g + i)
                    low, high = rope_a[i], rope_b[i]
                    pool.wait_ge(rope_link, e * ROPE_LINKS + 1)
                    nc.gpsimd.tensor_tensor(low[:], low[:], sin_sb[:], ALU.mult).then_inc(rope_sine, 1)
                    pool.wait_ge(rope_link, e * ROPE_LINKS + 4)
                    nc.gpsimd.tensor_tensor(low[:].bitcast(F32R), low[:], high[:], ALU.subtract).then_inc(rope_done, 1)

            def beside(b, last=False):
                if not isinstance(b, int) or b:
                    root(second_ln(b))
                rotate(b, 1)
                rotate(b, 2)
                if not last:
                    root(next_ln(b))
                rotate(b, 3)
                if not isinstance(b, int) or b:
                    root(third_ln(b, last))
                if not last:
                    rotate(b + 1, 0)

            root(0)
            pool.wait_ge(tables_loaded, 32)
            rotate(0, 0)
            beside(0)
            with pool.Fori(1, BATCHES - 1) as b:
                beside(b)
            beside(BATCHES - 1, last=True)
            root(BATCHES * 3 - 2)
            root(BATCHES * 3 - 1)
            pool.wait_ge(r_link, BATCHES * ROUTER_LINKS)
            pool.wait_ge(xn3_stored, 16 * BATCHES + 1)
            nc.gpsimd.memset(table_zero[:], 0).then_inc(consts_b, 1)
            nc.gpsimd.memset(tri[:], 1.0).then_inc(zeroed, 1)
            nc.gpsimd.memset(ones[:], 1.0).then_inc(consts_b, 1)
            nc.gpsimd.memset(zero_row[:], 0.0).then_inc(consts_b, 1)
            nc.gpsimd.iota(tok_i[:], pattern=[[P, TILES]], base=0, channel_multiplier=1).then_inc(consts_b, 1)
            nc.gpsimd.iota(steps[:], pattern=[[0, EXPERTS], [BT, BLOCKS - 1]], base=BT, channel_multiplier=0,
                           allow_small_or_imprecise_dtypes=True).then_inc(consts_b, 1)
            pool.wait_ge(zeroed, 4)
            nc.gpsimd.affine_select(out=tri[:], in_=tri[:], compare_op=ALU.is_ge, fill=0.0, base=-1,
                                    pattern=[[1, P]], channel_multiplier=-1).then_inc(consts_b, 1)
            pool.wait_ge(slots_ready, 1)
            pool.wait_ge(table_cleared, 16)
            for k in range(2):
                for t in range(TILES):
                    pool.indirect_dma_start(out=token_d, out_offset=bass.IndirectOffsetOnAxis(
                        ap=place_i[:, k, t:t + 1], axis=0), in_=tok_i[:, t:t + 1], in_offset=None)\
                        .then_inc(table_written, 16)
            pool.wait_ge(table_written, 16 * 2 * TILES)
            pool.dma_start(table[:], token_d.rearrange("(p n) o -> p (n o)", p=P)).then_inc(table_loaded, 16)
            pool.wait_ge(table_loaded, 16)

            def gather(block):
                nc.gpsimd.tensor_copy(table_cur[:], table[:, bass.ds(block * BA, BA)]).then_inc(cur_copied, 1)
                pool.wait_ge(cur_copied, block + 1)
                pass_wait(pool)
                for a in range(BA):
                    pool.indirect_dma_start(out=routed.x[:, a, :], out_offset=None, in_=xn3_d,
                                            in_offset=bass.IndirectOffsetOnAxis(ap=table_cur[:, a:a + 1], axis=0))\
                        .then_inc(routed.x_loaded, 16)

            gather(0)
            with pool.Fori(0, EXPERTS // 2) as pair:
                for k in range(2):
                    e = pair * 2 + k
                    lo, hi = block_range(pool, e)
                    with pool.Fori(lo, hi) as j:
                        pool.wait_ge(routed.x_turned, j * BA + BA)
                        pass_wait(pool)
                        gather(j + 1)
            pool.wait_ge(y_stored, (ROUTED_BLOCKS + 1) * 16 + 16)
            with pool.Fori(0, BLOCKS) as j:
                pool.wait_ge(picked_used[0], j + 1)
                pool.wait_ge(picked_used[1], j + 1)
                pass_wait(pool)
                nc.gpsimd.tensor_copy(pick_i[:], slot_i[:, :, bass.ds(j * BA, BA)]).then_inc(pick_copied, 1)
                pool.wait_ge(pick_copied, j + 1)
                pass_wait(pool)
                for a in range(BA):
                    for k in range(2):
                        pool.indirect_dma_start(out=picked[:, a, k, :], out_offset=None, in_=y_d,
                                                in_offset=bass.IndirectOffsetOnAxis(ap=pick_i[:, k, a:a + 1], axis=0))\
                            .then_inc(pick_loaded[a], 16)

        @block.scalar
        def _(act):
            def copy_turned(dst, ln, tiles, banks=(X_BANK, X_BANK + 1)):
                for t in tiles:
                    act.wait_ge(ln_tr, ln * TT + t + 1)
                    nc.scalar.copy(dst[:, :, t * P:(t + 1) * P],
                                   ps[:, banks[t % 2], :].rearrange("p (c n) -> p c n", c=CC)).then_inc(ln_xnT, 1)

            def exponentials(b, n, h):
                w = (n % TT + 1) * P
                if h == 0:
                    act.wait_ge(nb_done, b * STEPS + n + 1)
                pr = probs[n % TT][:, h, 0:w]
                nc.scalar.activation(pr, pr, ACT.Exp, bias=nb[:, n % 2, h:h + 1], scale=SCALE,
                                     accum_out=sums[:, n % 2, h:h + 1]).then_inc(exp_done, 1)

            def copy_probsT(b, n, h):
                w = (n % TT + 1) * P
                if n >= 2 and h == 0:
                    act.wait_ge(pv_mm, b * STEPS + n - 1)
                act.wait_ge(pT_mm, b * HEADS * TT + GH * n + h + 1)
                nc.scalar.copy(probsT[n % 2][:, h, 0:w], ps[:, T_BANK + h % 2, 0:w]).then_inc(pT_done, 1)

            def copy_yT(b, n):
                if n % TT == TT - 1:
                    act.wait_ge(pv_mm, b * STEPS + n + 1)
                    nc.scalar.copy(yT[:, n // TT, :], ps[:, O_BANK, :]).then_inc(yT_done, 1)

            def cross(p, ln2, ln3, place):
                if place - 1 in CTX_QK:
                    i = CTX_QK[place - 1]
                    act.wait_ge(qk2_mm, p * 2 + i + 1)
                    nc.scalar.activation((q2, k2)[i][:], ps[:, X_BANK + i, :], ACT.Identity, bias=bias_sb[:, i:i + 1],
                                         scale=1.0).then_inc(qk2_done, 1)
                copy_turned(xn_xT, ln2, LN2_TURNS.get(place - 1, ()))
                for t in ENERGIES.get(place - E_EXP, ()):
                    act.wait_ge(e_nb, p * TT + t + 1)
                    nc.scalar.activation(att[:, t % 2, :], ps[:, X_BANK + t % 2, :], ACT.Exp, bias=a_nb[:, t:t + 1],
                                         scale=1.0, accum_out=a_sums[:, t:t + 1]).then_inc(e_exp, 1)
                for t in ENERGIES.get(place - E_COPY, ()):
                    act.wait_ge(aT_mm, p * TT + t + 1)
                    nc.scalar.copy(attT[:, :, t * P:(t + 1) * P],
                                   ps[:, X_BANK + t % 2, :].rearrange("p (c n) -> p c n", c=TT)).then_inc(aT_done, 1)
                copy_turned(xn_xT, ln3, LN3_TURNS.get(place - 1, ()))
                if place == route_place(p):
                    act.wait_ge(r_shift, p + 1)
                    nc.scalar.activation(r_sc[:], r_t[:], ACT.Exp).then_inc(r_exp, 1)

            def high_part(n, buf, i):
                src, dst = weight_chunks(gu_raw, d_raw)[i], weight_chunks(gu_hi[buf], d_hi[buf])[i]
                nc.scalar.copy(dst, src).then_inc(hi_made, 1)

            def copy_values(b, place):
                if place in VALUE_COPIES:
                    t = VALUE_COPIES[place]
                    act.wait_ge(v_mm, b * TT + t + 1)
                    nc.scalar.copy(v_sb[:, t, :], ps[:, V_BANKS[t], :]).then_inc(v_done, 1)

            def attend(b, p, last=False):
                if p is None:
                    for place in range(STEPS):
                        copy_values(b, place)
                for r in range(STEPS + WEIGH_LAG):
                    for h in range(GH):
                        if 0 <= r - EXP_LAG < STEPS:
                            exponentials(b, r - EXP_LAG, h)
                        if 0 <= r - TURN_LAG < STEPS:
                            copy_probsT(b, r - TURN_LAG, h)
                        place = GH * r + h
                        if p is not None:
                            copy_values(b, place)
                        if p is not None:
                            cross(p, second_ln(b), third_ln(b, last), place)
                        if place - 1 in NEXT_TURNS and not last:
                            act.wait_ge(qk_mm, b * (2 * GROUPS) + 2 * GROUPS)
                            copy_turned(xnT, next_ln(b), (NEXT_TURNS[place - 1],), (NEXT_BANK, NEXT_BANK))
                        if place in SPLIT_PLACES and last:
                            if place == SPLIT_PLACES[0]:
                                act.wait_ge(raw_loaded, RAW)
                                act.wait_ge(stacked, BATCHES * GROUPS * STACK)
                            high_part(0, 0, SPLIT_PLACES.index(place))
                    if 0 <= r - WEIGH_LAG < STEPS:
                        copy_yT(b, r - WEIGH_LAG)

            copy_turned(xnT, 0, range(TT))
            attend(0, None)
            act.wait_ge(w_loaded, 16 * W_LOADS)
            with act.Fori(1, BATCHES - 1) as b:
                attend(b, b - 1)
            attend(BATCHES - 1, BATCHES - 2, last=True)

            def split(n, buf):
                act.wait_ge(slot_done, n - 1)
                act.wait_ge(raw_loaded, n * RAW + RAW)
                for i in range(WC):
                    high_part(n, buf, i)

            def turn(path, block):
                for a in range(BA):
                    act.wait_ge(path.x_turned, block * BA + a + 1)
                    nc.scalar.copy(path.xT_hi[:, :, a * P:(a + 1) * P],
                                   ps[:, XT_BANK + a, :].rearrange("p (c n) -> p c n", c=CC)).then_inc(path.xT_hi_done, 1)

            def silu_chunk(path, j, f):
                fn = HCHUNKS[f][1]
                act.wait_ge(path.gu_mm, j * NF + f + 1)
                nc.scalar.activation(sg[0:fn, f, :], ps[0:fn, f, 0:BT], ACT.Silu).then_inc(path.sg_done, 1)

            def hidden_high(path, j, f):
                fn = HCHUNKS[f][1]
                act.wait_ge(path.h_done, j * NF + NF + f + 1)
                nc.scalar.copy(h_hi[0:fn, f, :], hf[0:fn, f, :]).then_inc(path.h_hi_done, 1)

            def silu(path, j):
                for f in range(NF + 1):
                    if f < NF:
                        silu_chunk(path, j, f)
                    if f >= 1:
                        hidden_high(path, j, f - 1)
                turn(path, j + 1)

            turn(shared, 0)
            for place in range(EARLY_PLACES):
                for half in range(2):
                    cross(BATCHES - 1, END_LN, END_LN + 1, 2 * place + half)
                for j, f in early(place, later(EARLY_GU, 1)):
                    silu_chunk(shared, j, f)
                for j, f in early(place, later(EARLY_GU, 2)):
                    hidden_high(shared, j, f)
                for j, _ in early(place, {EARLY_TURN + 1: 0}):
                    turn(shared, j + 1)
            for j in range(EARLY_BLOCKS, EARLY_BLOCKS + 2):
                silu(shared, j)
            act.wait_ge(raw_loaded, 2 * RAW)
            for i in range(WC):
                high_part(1, 1, i)
            with act.Fori(EARLY_BLOCKS + 2, BLOCKS) as j:
                silu(shared, j)
            turn(routed, 0)
            act.wait_ge(slots_ready, 1)
            with act.Fori(0, EXPERTS // 2) as pair:
                for k in range(2):
                    split(pair * 2 + (k + 2), k)
                    lo, hi = block_range(act, pair * 2 + k)
                    with act.Fori(lo, hi) as j:
                        silu(routed, j)
            with act.Fori(BLOCKS, 2 * BLOCKS) as j:
                silu(shared, j)

        @block.tensor
        def _(pe):
            pe.wait_ge(consts, 3)

            def turn_tile(ln, t, src, bank):
                for c in range(CC):
                    last = nc.tensor.transpose(ps[:, bank, c * P:(c + 1) * P], src[:, t, c * P:(c + 1) * P], ident[:])
                last.then_inc(ln_tr, 1)

            def turn_ln(ln, tiles, src, free):
                for t in tiles:
                    pe.wait_ge(ln_xn, ln * TT + t + 1)
                    if t < 2:
                        pe.wait_ge(free[t][0], free[t][1])
                    else:
                        pe.wait_ge(ln_xnT, ln * TT + t - 1)
                    turn_tile(ln, t, src, X_BANK + t % 2)

            def turn_next(b, t):
                ln = next_ln(b)
                pe.wait_ge(ln_xn, ln * TT + t + 1)
                if t == 0:
                    pe.wait_ge(qk_used, b * (2 * GROUPS) + 2 * GROUPS)
                else:
                    pe.wait_ge(ln_xnT, ln * TT + t)
                turn_tile(ln, t, xn1, NEXT_BANK)

            def project_qk(b, g, i, chunks):
                e = 2 * g + i
                if chunks[0] == 0 and (not isinstance(b, int) or b or e):
                    pe.wait_ge(qk_used, b * (2 * GROUPS) + e)
                for c in chunks:
                    col = i * DIM + g * P
                    last = nc.tensor.matmul(ps[:, QK_BANK, :], wa_sb[:, c, col:col + P], xnT[:, c, :],
                                            start=(c == 0), stop=(c == CC - 1))
                if CC - 1 in chunks:
                    last.then_inc(qk_mm, 1)

            def scores(b, n, h):
                g, i = divmod(n, TT)
                w = max((i + 1) * P, 2 * P)
                if h == 0:
                    pe.wait_ge(stacked, b * (GROUPS * STACK) + (g + 1) * STACK)
                if n or h >= 2:
                    pe.wait_ge(s_masked, b * HEADS * TT + GH * n + h - 1)
                nc.tensor.matmul(ps[:, S_BANK + h % 2, 0:w], qs[:, g % 2, h, i * P:(i + 1) * P],
                                 ks[:, g % 2, h, 0:w],
                                 start=True, stop=True).then_inc(s_mm, 1)

            def turn_probs(b, n, h):
                pe.wait_ge(p_ready, b * HEADS * TT + GH * n + h + 1)
                if n or h >= 2:
                    pe.wait_ge(pT_done, b * HEADS * TT + GH * n + h - 1)
                for j in range(n % TT + 1):
                    last = nc.tensor.transpose(ps[:, T_BANK + h % 2, j * P:(j + 1) * P],
                                               probs[n % TT][:, h, j * P:(j + 1) * P], ident[:])
                last.then_inc(pT_mm, 1)

            def weigh(b, n, j):
                g, i = divmod(n, TT)
                if j == 0:
                    pe.wait_ge(pT_done, b * HEADS * TT + GH * n + GH)
                    if i == 0 and g >= 1:
                        pe.wait_ge(yT_done, b * GROUPS + g)
                for h in range(GH):
                    last = nc.tensor.matmul(ps[h * HDIM:(h + 1) * HDIM, O_BANK, i * P:(i + 1) * P],
                                            v_sb[:, j, g * P + h * HDIM:g * P + (h + 1) * HDIM],
                                            probsT[n % 2][:, h, j * P:(j + 1) * P],
                                            start=(j == 0), stop=(j == i), skip_group_check=True)
                if j == i:
                    last.then_inc(pv_mm, 1)

            def project_out(b, t, g):
                out_mm = nc.tensor.matmul(ps[:, PROJ_BANKS[t], :], yT[:, g, t * P:(t + 1) * P], wp_sb[:, g, :],
                                          start=(g == 0), stop=(g == GROUPS - 1))
                if g == GROUPS - 1:
                    out_mm.then_inc(proj_mm, 1)

            def project_last(p):
                pe.wait_ge(yT_done, p * GROUPS + GROUPS)
                for t in range(TT):
                    project_out(p, t, GROUPS - 1)

            def cross(p, ln2, ln3, place):
                if place in CTX_QK:
                    i = CTX_QK[place]
                    w = (wq_sb, wk_sb)[i]
                    pe.wait_ge(ctx_loaded, p * 16 + 16)
                    pe.wait_ge(proj_added, p * TT + TT)
                    for c in range(NCTX):
                        last = nc.tensor.matmul(ps[:, X_BANK + i, :], w[:, c, :], ctx_sb[:, c, :],
                                                start=(c == 0), stop=(c == NCTX - 1))
                    last.then_inc(qk2_mm, 1)
                turn_ln(ln2, LN2_TURNS.get(place, ()), xn, [(qk2_done, p * 2 + 1), (qk2_done, p * 2 + 2)])
                for t in ENERGIES.get(place, ()):
                    if t < 2:
                        pe.wait_ge(ln_xnT, ln2 * TT + TT)
                    else:
                        pe.wait_ge(aT_done, p * TT + t - 1)
                    nc.tensor.matmul(ps[:, X_BANK + t % 2, :], q2[:, t * P:(t + 1) * P], k2[:], start=True, stop=True)\
                        .then_inc(e_mm, 1)
                for t in ENERGIES.get(place - E_TURN, ()):
                    pe.wait_ge(a_ready, p * TT + t + 1)
                    for c in range(TT):
                        last = nc.tensor.transpose(ps[:, X_BANK + t % 2, c * P:(c + 1) * P],
                                                   att[:, t % 2, c * P:(c + 1) * P], ident[:])
                    last.then_inc(aT_mm, 1)
                if place in MIXES:
                    t, c = MIXES[place]
                    if c == 0 and t < 2:
                        pe.wait_ge(aT_done, p * TT + TT)
                    elif c == 0:
                        pe.wait_ge(xm_added, p * TT + t - 1)
                    mix = nc.tensor.matmul(ps[:, X_BANK + t % 2, :], xn_xT[:, c, t * P:(t + 1) * P], attT[:, c, :],
                                           start=(c == 0), stop=(c == TT - 1))
                    if c == TT - 1:
                        mix.then_inc(xm_mm, 1)
                turn_ln(ln3, LN3_TURNS.get(place, ()), xn, [(xm_added, p * TT + TT - 1), (xm_added, p * TT + TT)])
                if place in ROUTES:
                    t = ROUTES[place]
                    pe.wait_ge(ln_xnT, ln3 * TT + TT)
                    for c in range(CC):
                        last = nc.tensor.matmul(ps[:, X_BANK, t * EXPERTS:(t + 1) * EXPERTS],
                                                xn_xT[:, c, t * P:(t + 1) * P], wr_sb[:, c, :],
                                                start=(c == 0), stop=(c == CC - 1))
                    if t == TT - 1:
                        last.then_inc(r_mm, 1)

            def values(b, place):
                if place in VALUES:
                    t, chunks = VALUES[place]
                    if place == 3 * (TT - 1):
                        pe.wait_ge(v_done, b * TT + 1)
                    for c in chunks:
                        v = nc.tensor.matmul(ps[:, V_BANKS[t], :], xnT[:, c, t * P:(t + 1) * P],
                                             wa_sb[:, c, 2 * DIM:3 * DIM], start=(c == 0), stop=(c == CC - 1))
                    if CC - 1 in chunks:
                        v.then_inc(v_mm, 1)

            def attend(b, p, last=False):
                if p is None:
                    pe.wait_ge(ln_xnT, TT)
                else:
                    project_last(p)
                if p is None:
                    for place in range(STEPS):
                        values(b, place)
                for r in range(STEPS + WEIGH_LAG):
                    if r == 0 and p is not None:
                        pe.wait_ge(proj_added, p * TT + 2)
                    if r == TURN_LAG:
                        pe.wait_ge(v_done, b * TT + (TT - 1))
                    if r == WEIGH_LAG:
                        pe.wait_ge(v_done, b * TT + TT)
                    for h in range(GH):
                        if r < STEPS:
                            scores(b, r, h)
                        if 0 <= r - WEIGH_LAG < STEPS and h <= (r - WEIGH_LAG) % TT:
                            weigh(b, r - WEIGH_LAG, h)
                        if 0 <= r - TURN_LAG < STEPS:
                            turn_probs(b, r - TURN_LAG, h)
                        place = GH * r + h
                        if p is not None:
                            values(b, place)
                        if place in PROJECTIONS:
                            t, g = PROJECTIONS[place]
                            if g == 0 and t == 0:
                                if p is None:
                                    pe.wait_ge(w_loaded, 16 * W_LOADS)
                                pe.wait_ge(s_masked, b * (HEADS * TT) + HEADS * TT)
                                pe.wait_ge(yT_done, b * GROUPS + (GROUPS - 1))
                            if g == 0 and t == 2 and p is not None:
                                pe.wait_ge(r_shift, p + 1)
                                pe.wait_ge(ln_xnT, third_ln(b, last) * TT + TT)
                            project_out(b, t, g)
                        if place == NEXT_QK and not last:
                            pe.wait_ge(ln_xnT, next_ln(b) * TT + TT)
                        for what in queries_keys(place, b, last, QK_PLACES):
                            project_qk(*what)
                        if p is not None:
                            cross(p, second_ln(b), third_ln(b, last), place)
                        if place in NEXT_TURNS and not last:
                            turn_next(b, NEXT_TURNS[place])

            turn_ln(0, range(TT), xn1, [(consts, 3), (consts, 3)])
            pe.wait_ge(wa_loaded, 16)
            pe.wait_ge(ln_xnT, TT)
            for i in range(2):
                project_qk(0, 0, i, range(CC))
            attend(0, None)
            pe.wait_ge(w_loaded, 16 * W_LOADS)
            with pe.Fori(1, BATCHES - 1) as b:
                attend(b, b - 1)
            attend(BATCHES - 1, BATCHES - 2, last=True)
            project_last(BATCHES - 1)
            def turn(path, block):
                pe.wait_ge(path.x_loaded, block * (16 * path.loads) + 16 * path.loads)
                for a in range(BA):
                    for c in range(CC):
                        last = nc.tensor.transpose(ps[:, XT_BANK + a, c * P:(c + 1) * P], path.x[:, a, c * P:(c + 1) * P],
                                                   ident[:])
                    last.then_inc(path.x_turned, 1)

            def gate_up(path, j, buf, f):
                f0, fn = HCHUNKS[f]
                pe.wait_ge(path.h_done, j * NF + f + 1)
                for m in range(2):
                    terms = [(w, xT, m * CC + c, c) for w, xT in ((gu_hi[buf], path.xT_hi), (gu_lo[buf], path.xT_hi),
                                                                  (gu_hi[buf], path.xT_lo)) for c in range(CC)]
                    for i, (w, xT, r, c) in enumerate(terms):
                        last = nc.tensor.matmul(ps[0:fn, f, m * BT:(m + 1) * BT], w[:, r, f0:f0 + fn], xT[:, c, :],
                                                start=(i == 0), stop=(i == len(terms) - 1))
                last.then_inc(path.gu_mm, 1)

            def down(buf, f, a, bank):
                fn = HCHUNKS[f][1]
                for i, (h, w) in enumerate(((h_hi, d_hi[buf]), (h_hi, d_lo[buf]), (h_lo, d_hi[buf]))):
                    last = nc.tensor.matmul(ps[:, bank, :], h[0:fn, f, a * P:(a + 1) * P], w[0:fn, f, :],
                                            start=(f == 0 and i == 0), stop=(f == NF - 1 and i == 2),
                                            skip_group_check=True)
                return last

            def expert(path, j, buf):
                pe.wait_ge(path.xT_done, j * BA + BA)
                for f in range(NF):
                    gate_up(path, j, buf, f)
                turn(path, j + 1)
                pe.wait_ge(path.y_out, j * BA + BA)
                for f in range(NF):
                    pe.wait_ge(path.hT_done, j * NF + f + 1)
                    for a in range(BA):
                        last = down(buf, f, a, Y_BANK + a)
                        if f == NF - 1:
                            last.then_inc(path.y_mm, 1)

            turn(shared, 0)
            for place in range(EARLY_PLACES):
                for half in range(2):
                    cross(BATCHES - 1, END_LN, END_LN + 1, 2 * place + half)
                if place == COUNT_PLACE:
                    pe.wait_ge(consts_b, 6)
                    pe.wait_ge(both_done, 1)
                    flat = both[:].rearrange("p t e -> p (t e)")
                    nc.tensor.matmul(ps[:, COUNT_BANK, 0:P], tri[:], flat, start=True, stop=True)
                    nc.tensor.matmul(ps[:, COUNT_BANK, P:2 * P], ones[:], flat, start=True, stop=True)\
                        .then_inc(count_mm, 1)
                for j, f in early(place, EARLY_GU):
                    if f == 0:
                        pe.wait_ge(lo_made, WC)
                        pe.wait_ge(shared.xT_done, j * BA + BA)
                    gate_up(shared, j, 0, f)
                for j, _ in early(place, {EARLY_TURN: 0}):
                    turn(shared, j + 1)
                for j, a in early(place, EARLY_Y):
                    pe.wait_ge(shared.hT_done, j * NF + NF)
                    pe.wait_ge(shared.y_out, j * BA + (BA + a))
                    for f in range(NF):
                        last = down(0, f, a, Y_BANK)
                    last.then_inc(shared.y_mm, 1)
            with pe.Fori(EARLY_BLOCKS, BLOCKS) as j:
                expert(shared, j, 0)
            pe.wait_ge(shared.xT_done, (BLOCKS + 1) * BA)
            turn(routed, 0)
            pe.wait_ge(shared.y_out, (BLOCKS + 1) * BA)
            pe.wait_ge(slots_ready, 1)
            with pe.Fori(0, EXPERTS // 2) as pair:
                for k in range(2):
                    pe.wait_ge(lo_made, pair * (2 * WC) + WC * (k + 2))
                    pass_wait(pe)
                    lo, hi = block_range(pe, pair * 2 + k)
                    with pe.Fori(lo, hi) as j:
                        expert(routed, j, 1 - k)
            total = pe.value_load(first_i[0:1, EXPERTS:EXPERTS + 1], min_val=1, max_val=ROUTED_BLOCKS)
            pe.wait_ge(routed.xT_done, total * BA + BA)
            pe.wait_ge(routed.y_out, total * BA + BA)
            pass_wait(pe)
            pe.wait_ge(lo_made, SLOTS * WC)
            with pe.Fori(BLOCKS, 2 * BLOCKS) as j:
                expert(shared, j, 1)

        @block.vector
        def _(dve):
            dve.nop().then_inc(xn3_stored, 1)
            dve.wait_ge(x_loaded, 16)
            dve.wait_ge(consts, 3)

            def tile_stats(b, ln, t):
                nc.vector.bn_stats(stats[:, t, :], acc[:, bass.ds(b * TT + t, 1), :]
                                   .rearrange("p o d -> p (o d)")).then_inc(ln_stats, 1)

            def variances(ln):
                per = 2 * TT
                dve.wait_ge(ln_stats, ln * per + TT)
                pass_wait(dve)
                for t in range(TT):
                    nc.vector.bn_aggr(mv[:, t, :], stats[:, t, :]).then_inc(ln_stats, 1)
                dve.wait_ge(ln_stats, ln * per + per)
                nc.vector.tensor_scalar(veps[:], mv[:, :, 1], EPS, None, ALU.add).then_inc(ln_var, 1)

            def scale(dst, b, ln, t):
                if t == 0:
                    if not isinstance(ln, int) or ln:
                        dve.wait_ge(ln_tr, ln * TT)
                    dve.wait_ge(ln_rstd, ln + 1)
                nc.vector.tensor_scalar(dst[:, t, :], acc[:, bass.ds(b * TT + t, 1), :]
                                        .rearrange("p o d -> p (o d)"), mv[:, t, 0:1], rstd[:, t:t + 1],
                                        ALU.subtract, ALU.mult).then_inc(ln_xn, 1)

            swap = [i ^ 1 for i in range(32)]

            def rope(b, g, i, steps):
                e = 2 * g + i
                links = b * (2 * GROUPS * ROPE_LINKS) + e * ROPE_LINKS
                raw, low, high = ps[:, QK_BANK, :], rope_a[i], rope_b[i]
                if 0 in steps:
                    if not isinstance(b, int) or b or g:
                        dve.wait_ge(stacked, b * (GROUPS * STACK) + g * STACK)
                    dve.wait_ge(qk_mm, b * (2 * GROUPS) + e + 1)
                    pass_wait(dve)
                    nc.vector.stream_shuffle(low[:], raw, swap).then_inc(rope_link, 1)
                    nc.vector.tensor_tensor(high[:], raw, cos_sb[:], ALU.mult).then_inc(rope_link, 1)
                    dve.wait_ge(rope_link, links + 2)
                    dve.nop().then_inc(qk_used, 1)
                if 1 in steps:
                    dve.wait_ge(rope_sine, b * (2 * GROUPS) + (e + 1))
                    nc.vector.tensor_tensor(low[:], low[:], high[:], ALU.add).then_inc(rope_link, 1)
                    dve.wait_ge(rope_link, links + 3)
                    nc.vector.tensor_copy(high[:].bitcast(F32R), low[:]).then_inc(rope_link, 1)

            def mask_and_max(b, n, h):
                i = n % TT
                w = (i + 1) * P
                dve.wait_ge(s_mm, b * HEADS * TT + GH * n + h + 1)
                if n >= WEIGH_LAG:
                    dve.wait_ge(pT_mm, b * HEADS * TT + GH * (n - WEIGH_LAG) + h + 1)
                pass_wait(dve)
                nc.vector.tensor_tensor_reduce(probs[n % TT][:, h, 0:w], ps[:, S_BANK + h % 2, 0:w],
                                               mask[:, TOKENS - w:], 1.0, LOWEST, ALU.add, ALU.max,
                                               mx[:, n % 2, h:h + 1]).then_inc(s_masked, 1)
                if h == GH - 1:
                    dve.wait_ge(s_masked, b * HEADS * TT + GH * n + GH)
                    nc.vector.tensor_scalar(nb[:, n % 2, :], mx[:, n % 2, :], -SCALE, None, ALU.mult).then_inc(nb_done, 1)

            def divide(b, n, h):
                w = (n % TT + 1) * P
                if h == 0:
                    dve.wait_ge(exp_done, b * HEADS * TT + GH * n + GH)
                    nc.vector.reciprocal(rsum[:, n % 2, :], sums[:, n % 2, :]).then_inc(rsum_done, 1)
                    dve.wait_ge(rsum_done, b * STEPS + n + 1)
                pr = probs[n % TT][:, h, 0:w]
                nc.vector.tensor_scalar(pr, pr, rsum[:, n % 2, h:h + 1], None, ALU.mult).then_inc(p_ready, 1)

            def add_to_residual(b, t, bank, ready, added):
                dve.wait_ge(ready, b * TT + t + 1)
                tile = acc[:, bass.ds(b * TT + t, 1), :].rearrange("p o d -> p (o d)")
                nc.vector.tensor_tensor(tile, tile, ps[:, bank, :], ALU.add).then_inc(added, 1)

            def after_projection(p, ln):
                for t in range(TT):
                    add_to_residual(p, t, PROJ_BANKS[t], proj_mm, proj_added)
                    dve.wait_ge(proj_added, p * TT + t + 1)
                    pass_wait(dve)
                    tile_stats(p, ln, t)
                variances(ln)

            def route(b):
                count = [0]

                def link(ins):
                    count[0] += 1
                    ins.then_inc(r_link, 1)
                    dve.wait_ge(r_link, b * ROUTER_LINKS + count[0])

                def wide(m):
                    return m.unsqueeze(2).to_broadcast([P, TT, EXPERTS])

                logits = ps[:, X_BANK, 0:TT * EXPERTS].rearrange("p (t e) -> p t e", e=EXPERTS)
                dve.wait_ge(r_mm, b + 1)
                link(nc.vector.tensor_reduce(r_m[:], logits, AX_X, ALU.max))
                nc.vector.tensor_tensor(r_t[:], logits, wide(r_m[:]), ALU.subtract).then_inc(r_shift, 1)
                dve.wait_ge(r_exp, b + 1)
                link(nc.vector.tensor_reduce(r_m[:], r_sc[:], AX_X, ALU.add))
                link(nc.vector.reciprocal(r_m[:], r_m[:]))
                link(nc.vector.tensor_tensor(r_sc[:], r_sc[:], wide(r_m[:]), ALU.mult))

                def pick(k, values, scratch):
                    tiles = bass.ds(b * TT, TT)
                    link(nc.vector.tensor_reduce(r_m[:], values, AX_X, ALU.max))
                    link(nc.vector.tensor_copy(weight[:, k, tiles], r_m[:]))
                    link(nc.vector.tensor_tensor(scratch, values, wide(r_m[:]), ALU.is_lt))
                    link(nc.vector.scalar_tensor_tensor(out=scratch, in0=scratch, scalar=float(EXPERTS),
                                                        in1=iota8[:], op0=ALU.mult, op1=ALU.add))
                    link(nc.vector.tensor_reduce(r_m[:], scratch, AX_X, ALU.min))
                    link(nc.vector.tensor_tensor(r_oh[:], iota8[:], wide(r_m[:]), ALU.is_equal))
                    link(nc.vector.tensor_copy(onehot[:, k, tiles, :], r_oh[:]))

                pick(0, r_sc[:], r_t[:])
                link(nc.vector.scalar_tensor_tensor(out=r_t[:], in0=r_oh[:], scalar=-2.0, in1=r_sc[:],
                                                    op0=ALU.mult, op1=ALU.add))
                pick(1, r_t[:], r_t[:])
                assert count[0] == ROUTER_LINKS, count

            def cross(p, ln2, ln3, place):
                if place in LN2_SCALES:
                    if LN2_SCALES[place] == 0:
                        dve.wait_ge(xn3_stored, p * 16 + 1)
                    scale(xn, p, ln2, LN2_SCALES[place])
                for t in ENERGIES.get(place - E_MAX, ()):
                    dve.wait_ge(e_mm, p * TT + t + 1)
                    nc.vector.tensor_reduce(a_mx[:, t:t + 1], ps[:, X_BANK + t % 2, :], AX_X, ALU.max)\
                        .then_inc(e_max, 1)
                    dve.wait_ge(e_max, p * TT + t + 1)
                    nc.vector.tensor_scalar(a_nb[:, t:t + 1], a_mx[:, t:t + 1], -1.0, None, ALU.mult)\
                        .then_inc(e_nb, 1)
                for t in ENERGIES.get(place - E_DIVIDE, ()):
                    dve.wait_ge(e_exp, p * TT + t + 1)
                    nc.vector.reciprocal(a_rsum[:, t:t + 1], a_sums[:, t:t + 1]).then_inc(e_rsum, 1)
                    dve.wait_ge(e_rsum, p * TT + t + 1)
                    nc.vector.tensor_scalar(att[:, t % 2, :], att[:, t % 2, :], a_rsum[:, t:t + 1], None,
                                            ALU.mult).then_inc(a_ready, 1)
                for t in MIX_ADDS.get(place, ()):
                    add_to_residual(p, t, X_BANK + t % 2, xm_mm, xm_added)
                if place in LN3_STATS:
                    dve.wait_ge(xm_added, p * TT + LN3_STATS[place] + 1)
                    pass_wait(dve)
                    tile_stats(p, ln3, LN3_STATS[place])
                if place == LN3_VARIANCE:
                    variances(ln3)
                if place in LN3_SCALES:
                    scale(xn, p, ln3, LN3_SCALES[place])
                if place == route_place(p):
                    route(p)

            def low_part(n, buf, i):
                dve.wait_ge(hi_made, n * WC + (i + 1))
                src, high, dst = (weight_chunks(gu, d)[i] for gu, d in
                                  ((gu_raw, d_raw), (gu_hi[buf], d_hi[buf]), (gu_lo[buf], d_lo[buf])))
                nc.vector.tensor_tensor(dst, src, high.bitcast(F32), ALU.subtract).then_inc(lo_made, 1)

            def attend(b, p, last=False):
                if p is not None:
                    after_projection(p, second_ln(b))
                for r in range(STEPS + WEIGH_LAG):
                    for h in range(GH):
                        if 0 <= r - DIVIDE_LAG < STEPS:
                            divide(b, r - DIVIDE_LAG, h)
                        if r < STEPS:
                            mask_and_max(b, r, h)
                        place = GH * r + h
                        for what in queries_keys(place, b, last, ROPE_PLACES):
                            rope(*what)
                        if p is not None:
                            cross(p, second_ln(b), third_ln(b, last), place)
                        if not last:
                            for t in NEXT_STATS.get(place, ()):
                                if t == 0 and p is None:
                                    dve.wait_ge(w_loaded, 16 * W_LOADS)
                                    pass_wait(dve)
                                tile_stats(b + 1, next_ln(b), t)
                            if place == NEXT_VARIANCE:
                                variances(next_ln(b))
                            if place in NEXT_SCALES:
                                scale(xn1, b + 1, next_ln(b), NEXT_SCALES[place])
                        if place in SPLIT_PLACES and last:
                            low_part(0, 0, SPLIT_PLACES.index(place))

            for t in range(TT):
                tile_stats(0, 0, t)
            variances(0)
            for t in range(TT):
                scale(xn1, 0, 0, t)
            dve.wait_ge(tables_loaded, 32)
            for i in range(2):
                rope(0, 0, i, range(2))
            attend(0, None)
            with dve.Fori(1, BATCHES - 1) as b:
                attend(b, b - 1)
            attend(BATCHES - 1, BATCHES - 2, last=True)
            for k in range(2):
                dve.nop().then_inc(picked_used[k], 1)
            for path in (shared, routed):
                dve.nop().then_inc(path.h_done, NF)
                dve.nop().then_inc(path.y_out, BA)
            dve.nop().then_inc(y_stored, 16)

            after_projection(BATCHES - 1, END_LN)


            count = [0]

            def link(ins):
                count[0] += 1
                ins.then_inc(d_link, 1)
                dve.wait_ge(d_link, count[0])

            within = ps[:, COUNT_BANK, 0:P].rearrange("p (t e) -> p t e", e=EXPERTS)

            def count_tokens():
                dve.wait_ge(xn3_stored, 16 * BATCHES + 1)
                nc.vector.tensor_tensor(both[:], onehot[:, 0], onehot[:, 1], ALU.add).then_inc(both_done, 1)
                link(nc.vector.memset(before[:, 0, :], 0.0))
                link(nc.vector.memset(first[:, 0:1], 0.0))
                dve.wait_ge(count_mm, 1)
                dve.wait_ge(consts_b, 6)
                sums_to = [before[:, 1:, :], tots[:]]
                link(nc.vector.tensor_copy(sums_to[0], ps[:, COUNT_BANK, P:2 * P]
                                           .rearrange("p (t e) -> p t e", e=EXPERTS)))
                for step in range(TILES.bit_length() - 1):
                    by = 1 << step
                    src, dst = sums_to[step % 2], sums_to[1 - step % 2]
                    count[0] += 1
                    nc.vector.tensor_copy(dst[:, 0:by, :], src[:, 0:by, :]).then_inc(d_link, 1)
                    link(nc.vector.tensor_tensor(dst[:, by:, :], src[:, by:, :], src[:, 0:TILES - by, :], ALU.add))

            def place_experts():
                link(nc.vector.tensor_tensor(more[:], before[:, TILES, :].unsqueeze(2)
                                             .to_broadcast([P, EXPERTS, BLOCKS - 1]), steps[:], ALU.is_gt))
                link(nc.vector.tensor_reduce(nblk[:], more[:], AX_X, ALU.add))
                link(nc.vector.tensor_scalar(nblk[:], nblk[:], 1.0, None, ALU.add))
                for e in range(EXPERTS):
                    link(nc.vector.tensor_tensor(first[:, e + 1:e + 2], first[:, e:e + 1], nblk[:, e:e + 1], ALU.add))
                link(nc.vector.tensor_copy(first_i[:], first[:]))
                link(nc.vector.tensor_scalar(first_row[:], first[:, 0:EXPERTS], float(BT), None, ALU.mult))
                link(nc.vector.tensor_tensor(row[:], within, before[:, 0:TILES, :], ALU.add))
                link(nc.vector.tensor_tensor(row[:], row[:], first_row[:].unsqueeze(1)
                                             .to_broadcast([P, TILES, EXPERTS]), ALU.add))
                for k in range(2):
                    link(nc.vector.tensor_tensor(both[:], onehot[:, k], row[:], ALU.mult))
                    link(nc.vector.tensor_reduce(row_k[:, k, :], both[:], AX_X, ALU.add))
                link(nc.vector.tensor_copy(slot_i[:], row_k[:]))
                link(nc.vector.tensor_scalar(place_lo[:], slot_i[:], P - 1, None, ALU.bitwise_and))
                link(nc.vector.tensor_scalar(place_hi[:], slot_i[:], P.bit_length() - 1, None,
                                             ALU.arith_shift_right))
                nc.vector.scalar_tensor_tensor(out=place_i[:], in0=place_lo[:], scalar=float(SLOT_COLS),
                                               in1=place_hi[:], op0=ALU.mult, op1=ALU.add).then_inc(slots_ready, 1)

            def turn(path, block):
                for a in range(BA):
                    dve.wait_ge(path.xT_hi_done, block * BA + a + 1)
                    cols = slice(a * P, (a + 1) * P)
                    nc.vector.tensor_tensor(path.xT_lo[:, :, cols], ps[:, XT_BANK + a, :].rearrange("p (c n) -> p c n", c=CC),
                                            path.xT_hi[:, :, cols].bitcast(F32), ALU.subtract).then_inc(path.xT_done, 1)

            def gate_by_up(path, j, f):
                fn = HCHUNKS[f][1]
                dve.wait_ge(path.sg_done, j * NF + f + 1)
                nc.vector.tensor_tensor(hf[0:fn, f, :], sg[0:fn, f, :], ps[0:fn, f, BT:2 * BT], ALU.mult)\
                    .then_inc(path.h_done, 1)

            def hidden_low(path, j, f):
                fn = HCHUNKS[f][1]
                dve.wait_ge(path.h_hi_done, j * NF + f + 1)
                nc.vector.tensor_tensor(h_lo[0:fn, f, :], hf[0:fn, f, :], h_hi[0:fn, f, :].bitcast(F32),
                                        ALU.subtract).then_inc(path.hT_done, 1)

            def expert(path, j, put):
                for f in range(NF + 1):
                    if f < NF:
                        gate_by_up(path, j, f)
                    if f >= 1:
                        hidden_low(path, j, f - 1)
                turn(path, j + 1)
                for a in range(BA):
                    dve.wait_ge(path.y_mm, j * BA + a + 1)
                    put(a)

            def tile_of(j, a):
                return acc[:, bass.ds(j * BA + a, 1), :].rearrange("p o d -> p (o d)")

            def adder(j, bank):
                def add(a):
                    tile = tile_of(j, a)
                    nc.vector.tensor_tensor(tile, tile, ps[:, bank(a), :], ALU.add).then_inc(shared.y_out, 1)
                return add

            turn(shared, 0)
            for place in range(EARLY_PLACES):
                for j, a in early(place, later(EARLY_Y, 1)):
                    dve.wait_ge(shared.y_mm, j * BA + a + 1)
                    adder(j, lambda a: Y_BANK)(a)
                for half in range(2):
                    cross(BATCHES - 1, END_LN, END_LN + 1, 2 * place + half)
                for j, f in early(place, later(EARLY_GU, 1)):
                    gate_by_up(shared, j, f)
                for j, f in early(place, later(EARLY_GU, 2)):
                    hidden_low(shared, j, f)
                for j, _ in early(place, {EARLY_TURN + 1: 0}):
                    turn(shared, j + 1)
                if place == COUNT_PLACE:
                    count_tokens()
                    place_experts()
            j = EARLY_BLOCKS
            expert(shared, j, adder(j, lambda a: Y_BANK + a))
            expert(shared, j + 1, adder(j + 1, lambda a: Y_BANK + a))
            for i in range(WC):
                low_part(1, 1, i)
            with dve.Fori(EARLY_BLOCKS + 2, BLOCKS) as j:
                expert(shared, j, adder(j, lambda a: Y_BANK + a))
            dve.nop().then_inc(slot_done, 1)
            turn(routed, 0)
            with dve.Fori(0, EXPERTS // 2) as pair:
                for k in range(2):
                    for i in range(WC):
                        low_part(pair * 2 + (k + 2), k, i)
                    lo, hi = block_range(dve, pair * 2 + k)
                    with dve.Fori(lo, hi) as j:
                        def store(a):
                            if a == 0:
                                dve.wait_ge(y_stored, j * 16 + 16)
                            nc.vector.tensor_copy(y_sb[:, a, :], ps[:, Y_BANK + a, :]).then_inc(routed.y_out, 1)

                        expert(routed, j, store)
                    dve.nop().then_inc(slot_done, 1)
            dve.wait_ge(shared.y_out, (BLOCKS + 1) * BA)
            with dve.Fori(0, BLOCKS) as j:
                def add(a):
                    tile = tile_of(j, a)
                    nc.vector.tensor_tensor(tile, tile, ps[:, Y_BANK + a, :], ALU.add).then_inc(shared.y_out, 1)

                expert(shared, j + BLOCKS, add)
                dve.wait_ge(shared.y_out, j * BA + (BLOCKS + 2) * BA)
                for k in range(2):
                    for a in range(BA):
                        if k == 0:
                            dve.wait_ge(pick_loaded[a], j * 32 + 32)
                        tile = tile_of(j, a)
                        nc.vector.scalar_tensor_tensor(
                            out=tile, in0=picked[:, a, k, :], scalar=weight[:, k, bass.ds(j * BA + a, 1)], in1=tile,
                            op0=ALU.mult, op1=ALU.add).then_inc(acc_link, 1)
                    dve.wait_ge(acc_link, j * (2 * BA) + (k + 1) * BA)
                dve.nop().then_inc(tile_done, 1)
                for a in range(BA):
                    dve.nop().then_inc(picked_used[a], 1)


def rope_tables():
    theta = (1.0 / np.float32(10000.0) ** (np.arange(0, HDIM, 2, dtype=np.float32) / np.float32(HDIM))).astype(np.float32)
    angle = np.outer(np.arange(TOKENS, dtype=np.float32), theta).astype(np.float32)
    by_feature = np.repeat(np.arange(HDIM // 2), 2)
    sign = np.tile(np.array([-1.0, 1.0], np.float32), HDIM // 2)
    cos = np.cos(angle)[:, by_feature].T
    sin = (np.sin(angle)[:, by_feature] * sign).T
    return (np.ascontiguousarray(np.tile(cos, (GH, 1)), np.float32),
            np.ascontiguousarray(np.tile(sin, (GH, 1)), np.float32))


def kernel(**inputs):
    import concourse.bacc as _bacc
    from concourse.bass_utils import run_bass_kernel_spmd as _run

    i = {k: np.asarray(v) for k, v in inputs.items()}
    cos, sin = rope_tables()

    routed_gu = np.stack([i["L0_ffn_We_gate"], i["L0_ffn_We_up"]], axis=1)
    gate, up = (np.split(i[n], SHARED, axis=1) for n in ("L0_ffn_Ws_gate", "L0_ffn_Ws_up"))
    first_gu, second_gu = (np.stack([g, u])[None] for g, u in zip(gate, up))
    first_d, second_d = (d[None] for d in np.split(i["L0_ffn_Ws_down"], SHARED, axis=0))
    arrays = {
        "x": i["x"].reshape(BATCHES * TOKENS, DIM),
        "ctxT": i["ctx_1024"].transpose(0, 2, 1),
        "waT": i["L0_attn_w_atten"].T, "wpT": i["L0_attn_w_proj"].T,
        "wqT": i["L0_xattn_Wq"].T, "wkT": i["L0_xattn_Wk"].T,
        "bq": i["L0_xattn_bq"].reshape(P, 1), "bk": i["L0_xattn_bk"].reshape(P, 1),
        "wr": i["L0_ffn_W_router"],
        "we": np.concatenate([w.reshape(-1) for w in (first_gu, routed_gu, second_gu, first_d,
                                                      i["L0_ffn_We_down"], second_d)]),
        "cosT": cos, "sinT": sin,
    }
    arrays = {f"in_{k}": np.ascontiguousarray(v) for k, v in arrays.items()}
    nc = _bacc.Bacc("TRN2", target_bir_lowering=False, num_devices=1)
    args = [nc.dram_tensor(k, v.shape, mybir.dt.from_np(v.dtype), kind="ExternalInput").ap() for k, v in arrays.items()]
    out = nc.dram_tensor("out", (BATCHES * TOKENS, DIM), F32, kind="ExternalOutput").ap()
    build(nc, *args, out)
    r = _run(nc, [arrays], core_ids=[0])
    return r.results[0]["out"].reshape(BATCHES, TOKENS, DIM)
```
